# Optimizing a Trainium2 kernel written in Bass

```python
import numpy as np
import jax
import jax.numpy as jnp

def _softmax(x, axis=-1):
    return jax.nn.softmax(x, axis=axis)

def _gelu(x):
    return jax.nn.gelu(x, approximate=True)

def _silu(x):
    return jax.nn.silu(x)

def _sigmoid(x):
    return jax.nn.sigmoid(x)

def _layernorm(x, axis=-1, eps=1e-05):
    m = jnp.mean(x, axis=axis, keepdims=True)
    v = jnp.var(x, axis=axis, keepdims=True)
    return (x - m) / jnp.sqrt(v + eps)

def _scatter_add(tgt, idx, src, axis=0):
    return tgt.at[idx].add(src)

def _segment_sum(src, seg, n):
    return jax.ops.segment_sum(src, seg, n)
kernel_name = 'mk_flamingo_gated_d4_seqx_r4_8f46d0'

def setup_inputs(seed: int=0):
    np.random.seed(seed)
    _w = jnp.asarray

    def _rec_inputs():
        import jax
        import jax.numpy as jnp
        _rk = jax.random.key(seed)
        x = -1.394e-06 + 0.9999 * jax.random.normal(jax.random.fold_in(_rk, 1), (4, 512, 256), jnp.float32)
        _lenS = 512 - jax.random.randint(jax.random.fold_in(_rk, 7), (4,), 0, max(1, 512 // 4) + 1, jnp.int32)
        _lenS2 = 64 - jax.random.randint(jax.random.fold_in(_rk, 8), (4,), 0, max(1, 64 // 4) + 1, jnp.int32)
        _ctx_1024P = jax.random.normal(jax.random.fold_in(_rk, 11), (4, 16, 256), jnp.float32)
        _ctx_1024c = jax.random.dirichlet(jax.random.fold_in(_rk, 511), 0.3 * jnp.ones((16,), jnp.float32), (4, 64))
        _ctx_1024t = jnp.einsum('bsk,bkd->bsd', _ctx_1024c, _ctx_1024P)
        _ctx_1024t = _ctx_1024t * jax.lax.rsqrt(jnp.mean(jnp.square(_ctx_1024t)) + 1e-12) * 0.953939
        ctx_1024 = -0.000292821 + 1.00034 * (_ctx_1024t + 0.3 * jax.random.normal(jax.random.fold_in(_rk, 611), (4, 64, 256), jnp.float32))
        _validS = jnp.arange(512)[None, :] < _lenS[:, None]
        _validS2 = jnp.arange(64)[None, :] < _lenS2[:, None]
        _causal = jnp.tril(jnp.ones((512, 512), dtype=bool))
        mask_Bx1xSxS2_if1 = jnp.where(jnp.ones((4, 1, 512, 64), dtype=bool), 1, 0).astype(jnp.int32)
        mask_Bx1xS2_if1 = jnp.where(jnp.ones((4, 1, 64), dtype=bool), 1, 0).astype(jnp.int32)
        _g = jax.random.normal(jax.random.fold_in(_rk, 9001), (2, 4), jnp.float32)
        _g = jnp.sign(_g) * jnp.maximum(jnp.abs(_g), 1.0) + (_g == 0) * 1.0
        g_xattn = _g[0]
        g_ffn = _g[1]
        return (x, ctx_1024, mask_Bx1xSxS2_if1, mask_Bx1xS2_if1, g_xattn, g_ffn)
    x, ctx_1024, mask_Bx1xSxS2_if1, mask_Bx1xS2_if1, g_xattn, g_ffn = _rec_inputs()

    def _L0_xattn_setup():
        import jax, jax.numpy as jnp
        import numpy as np
        D_MODEL = 256
        HEADS = 16
        HEAD_DIM = D_MODEL // HEADS
        B, S = (2, 512)
        key0 = jax.random.key(seed)
        ks = jax.random.split(key0, 8)
        inp = {'key': jax.random.normal(ks[0], (B, S, D_MODEL), dtype=jnp.float32), 'query': jax.random.normal(ks[1], (B, S, D_MODEL), dtype=jnp.float32), 'value': jax.random.normal(ks[2], (B, S, D_MODEL), dtype=jnp.float32), 'mask': jnp.ones((B, 1, S, S), dtype=jnp.int32), 'Wq': jax.random.normal(ks[3], (D_MODEL, D_MODEL), dtype=jnp.float32) * 0.02, 'Wk': jax.random.normal(ks[4], (D_MODEL, D_MODEL), dtype=jnp.float32) * 0.02, 'Wv': jax.random.normal(ks[5], (D_MODEL, D_MODEL), dtype=jnp.float32) * 0.02, 'Wo': jax.random.normal(ks[6], (D_MODEL, D_MODEL), dtype=jnp.float32) * 0.02, 'bo': jax.random.normal(ks[7], (D_MODEL,), dtype=jnp.float32) * 0.02}
        return inp
    _L0_xattn_all = _L0_xattn_setup()
    _L0_xattn_in = {k: v for k, v in _L0_xattn_all.items() if k in ('Wq', 'Wk', 'Wv', 'Wo', 'bo')}
    del _L0_xattn_all

    def _L0_ffn_setup():
        import math
        import jax, jax.numpy as jnp
        import numpy as np
        B, S, H = (4, 512, 256)
        E, K, I = (8, 2, 256)
        NSH = 2
        CF, RSF = (1.25, 1.0)
        key = jax.random.key(seed)
        ks = jax.random.split(key, 8)
        w = lambda k, sh: jax.random.normal(k, sh, dtype=jnp.float32) * 0.02
        return {'hidden_states': jax.random.normal(ks[0], (B, S, H), dtype=jnp.float32), 'gate_w': w(ks[1], (E, H)), 'we_gate': w(ks[2], (E, I, H)), 'we_up': w(ks[3], (E, I, H)), 'we_down': w(ks[4], (E, H, I)), 'ws_gate': w(ks[5], (NSH * I, H)), 'ws_up': w(ks[6], (NSH * I, H)), 'ws_down': w(ks[7], (H, NSH * I))}
    _L0_ffn_all = _L0_ffn_setup()
    _L0_ffn_in = {k: v for k, v in _L0_ffn_all.items() if k in ('gate_w', 'we_gate', 'we_up', 'we_down', 'ws_gate', 'ws_up', 'ws_down')}
    del _L0_ffn_all

    def _L1_xattn_setup():
        import jax, jax.numpy as jnp
        import numpy as np
        B, S, E, H, W = (2, 1024, 256, 8, 8)

        def build_window_idx(seq_len):
            rows = []
            for t in range(seq_len):
                rp = [i for i in range(-4, 4) if 0 <= t + i < seq_len]
                while len(rp) < 8:
                    if t + len(rp) < seq_len:
                        rp.append(t + len(rp))
                    else:
                        rp.insert(0, t - (8 - len(rp)))
                rows.append([p % seq_len for p in rp])
            return np.asarray(rows, dtype=np.int32)
        key = jax.random.key(seed)
        ks = jax.random.split(key, 7)
        return {'q': jax.random.normal(ks[0], (B, S, E), jnp.float32), 'k': jax.random.normal(ks[1], (B, S, E), jnp.float32), 'v': jax.random.normal(ks[2], (B, S, E), jnp.float32), 'in_proj_w': jax.random.normal(ks[3], (3 * E, E), jnp.float32) * 0.02, 'in_proj_b': jax.random.normal(ks[4], (3 * E,), jnp.float32) * 0.02, 'out_w': jax.random.normal(ks[5], (E, E), jnp.float32) * 0.02, 'out_b': jax.random.normal(ks[6], (E,), jnp.float32) * 0.02}
    _L1_xattn_all = _L1_xattn_setup()
    _L1_xattn_in = {k: v for k, v in _L1_xattn_all.items() if k in ('in_proj_w', 'in_proj_b', 'out_w', 'out_b')}
    del _L1_xattn_all

    def _L1_ffn_setup():
        import jax, jax.numpy as jnp
        import numpy as np
        TOP_K = 2
        ROUTE_SCALE = 1.0
        EPS = 1e-20
        key = jax.random.key(seed)
        ks = jax.random.split(key, 8)
        dim, hid, E, X = (256, 704, 8, 1)
        std = 0.02
        x = jax.random.normal(ks[0], (2, 512, dim), dtype=jnp.float32)
        w1 = jax.random.normal(ks[1], (E, hid, dim), dtype=jnp.float32) * std
        w2 = jax.random.normal(ks[2], (E, dim, hid), dtype=jnp.float32) * std
        w3 = jax.random.normal(ks[3], (E, hid, dim), dtype=jnp.float32) * std
        new_w1 = jax.random.normal(ks[4], (X, hid, dim), dtype=jnp.float32) * std
        new_w2 = jnp.zeros((X, dim, hid), dtype=jnp.float32)
        new_w3 = jax.random.normal(ks[5], (X, hid, dim), dtype=jnp.float32) * std
        gate_weight = jax.random.normal(ks[6], (E, dim), dtype=jnp.float32) * std
        new_gate_weight = jax.random.normal(ks[7], (X, dim), dtype=jnp.float32) * std
        gate_bias = jnp.zeros((X,), dtype=jnp.float32)
        return dict(x=x, w1=w1, w2=w2, w3=w3, new_w1=new_w1, new_w2=new_w2, new_w3=new_w3, gate_weight=gate_weight, new_gate_weight=new_gate_weight, gate_bias=gate_bias)
    _L1_ffn_all = _L1_ffn_setup()
    _L1_ffn_in = {k: v for k, v in _L1_ffn_all.items() if k in ('w1', 'w2', 'w3', 'new_w1', 'new_w2', 'new_w3', 'gate_weight', 'new_gate_weight', 'gate_bias')}
    del _L1_ffn_all

    def _L2_xattn_setup():
        import jax, jax.numpy as jnp
        import numpy as np
        H = 256
        B = 8
        L_CHAR = 512
        L_SUB = 256

        def _linear(x, W, b):
            return jnp.einsum('blh,oh->blo', x, W) + b

        def _interp_linear(x, out_len):
            L_in = x.shape[1]
            pos = (jnp.arange(out_len, dtype=x.dtype) + 0.5) * (L_in / out_len) - 0.5
            pos = jnp.clip(pos, 0.0, L_in - 1)
            lo = jnp.floor(pos).astype(jnp.int32)
            hi = jnp.minimum(lo + 1, L_in - 1)
            w = (pos - lo.astype(x.dtype))[None, :, None]
            return x[:, lo] * (1 - w) + x[:, hi] * w
        key = jax.random.key(seed)
        ks = jax.random.split(key, 18)
        s = 0.02
        inp = {'char_emb': jax.random.normal(ks[0], (B, L_CHAR, H), jnp.float32), 'subword_emb': jax.random.normal(ks[1], (B, L_SUB, H), jnp.float32)}
        names = ['Wq_c', 'Wk_s', 'Wv_s', 'Wq_s', 'Wk_c', 'Wv_c']
        for i, n in enumerate(names):
            inp[n] = jax.random.normal(ks[2 + 2 * i], (H, H), jnp.float32) * s
            inp['b' + n[1:]] = jax.random.normal(ks[3 + 2 * i], (H,), jnp.float32) * s
        inp['Wg'] = jax.random.normal(ks[14], (H, 2 * H), jnp.float32) * s
        inp['bg'] = jax.random.normal(ks[15], (H,), jnp.float32) * s
        return inp
    _L2_xattn_all = _L2_xattn_setup()
    _L2_xattn_in = {k: v for k, v in _L2_xattn_all.items() if k in ('Wq_c', 'bq_c', 'Wk_s', 'bk_s', 'Wv_s', 'bv_s', 'Wq_s', 'bq_s', 'Wk_c', 'bk_c', 'Wv_c', 'bv_c', 'Wg', 'bg')}
    del _L2_xattn_all

    def _L2_ffn_setup():
        import jax, jax.numpy as jnp
        import numpy as np
        DIM = 256
        HID = 704
        E = 8
        TOP_K = 2
        EPS = 1e-06

        def _rmsnorm(x, w):
            var = jnp.mean(jnp.square(x), axis=-1, keepdims=True)
            return x * jax.lax.rsqrt(var + EPS) * w
        key = jax.random.key(seed)
        ks = jax.random.split(key, 5)
        x = jax.random.normal(ks[0], (4, 512, DIM), dtype=jnp.float32)
        norm_weight = jnp.ones((DIM,), dtype=jnp.float32)
        router_weight = jax.random.normal(ks[1], (E, DIM), dtype=jnp.float32) * 0.02
        gate_up_weight = jax.random.normal(ks[2], (E, 2 * HID, DIM), dtype=jnp.float32) * (0.02 / np.sqrt(E))
        down_weight = jax.random.normal(ks[3], (E, DIM, HID), dtype=jnp.float32) * (0.02 / np.sqrt(E))
        residual_alpha = jnp.float32(1.0)
        return {'x': x, 'norm_weight': norm_weight, 'router_weight': router_weight, 'gate_up_weight': gate_up_weight, 'down_weight': down_weight, 'residual_alpha': residual_alpha}
    _L2_ffn_all = _L2_ffn_setup()
    _L2_ffn_in = {k: v for k, v in _L2_ffn_all.items() if k in ('norm_weight', 'router_weight', 'gate_up_weight', 'down_weight', 'residual_alpha')}
    del _L2_ffn_all

    def _L3_xattn_setup():
        import jax, jax.numpy as jnp
        import numpy as np
        N_HEAD = 16
        N_FEAT = 256
        D_K = N_FEAT // N_HEAD
        key = jax.random.key(seed)
        ks = jax.random.split(key, 12)
        B, T, F = (4, 512, N_FEAT)
        s = 1.0 / np.sqrt(F)
        return {'query': jax.random.normal(ks[0], (B, T, F), dtype=jnp.float32), 'key': jax.random.normal(ks[1], (B, T, F), dtype=jnp.float32), 'value': jax.random.normal(ks[2], (B, T, F), dtype=jnp.float32), 'mask': jnp.ones((B, 1, T), dtype=jnp.int32), 'Wq': jax.random.normal(ks[3], (F, F), dtype=jnp.float32) * s, 'bq': jax.random.normal(ks[4], (F,), dtype=jnp.float32) * 0.01, 'Wk': jax.random.normal(ks[5], (F, F), dtype=jnp.float32) * s, 'bk': jax.random.normal(ks[6], (F,), dtype=jnp.float32) * 0.01, 'Wv': jax.random.normal(ks[7], (F, F), dtype=jnp.float32) * s, 'bv': jax.random.normal(ks[8], (F,), dtype=jnp.float32) * 0.01, 'Wo': jax.random.normal(ks[9], (F, F), dtype=jnp.float32) * s, 'bo': jax.random.normal(ks[10], (F,), dtype=jnp.float32) * 0.01}
    _L3_xattn_all = _L3_xattn_setup()
    _L3_xattn_in = {k: v for k, v in _L3_xattn_all.items() if k in ('Wq', 'bq', 'Wk', 'bk', 'Wv', 'bv', 'Wo', 'bo')}
    del _L3_xattn_all

    def _L3_ffn_setup():
        import jax, jax.numpy as jnp
        import numpy as np
        DIM = 256
        HIDDEN = 768
        SCALE = 1.0 / 127.0

        def _dequant(w_int, dtype):
            return w_int.astype(dtype) * jnp.asarray(SCALE, dtype)
        key = jax.random.key(seed)
        k_x, k_g, k_u, k_d = jax.random.split(key, 4)
        x = jax.random.normal(k_x, (4, 512, DIM), dtype=jnp.float32)
        w_gate = jax.random.randint(k_g, (HIDDEN, DIM), -127, 128, dtype=jnp.int32)
        w_up = jax.random.randint(k_u, (HIDDEN, DIM), -127, 128, dtype=jnp.int32)
        w_down = jax.random.randint(k_d, (DIM, HIDDEN), -127, 128, dtype=jnp.int32)
        return {'x': x, 'w_gate': w_gate, 'w_up': w_up, 'w_down': w_down}
    _L3_ffn_all = _L3_ffn_setup()
    _L3_ffn_in = {k: v for k, v in _L3_ffn_all.items() if k in ('w_gate', 'w_up', 'w_down')}
    del _L3_ffn_all
    return {'x': x, 'ctx_1024': ctx_1024, 'mask_Bx1xSxS2_if1': mask_Bx1xSxS2_if1, 'mask_Bx1xS2_if1': mask_Bx1xS2_if1, 'g_xattn': g_xattn, 'g_ffn': g_ffn, 'L0_xattn_Wq': _L0_xattn_in['Wq'], 'L0_xattn_Wk': _L0_xattn_in['Wk'], 'L0_xattn_Wv': _L0_xattn_in['Wv'], 'L0_xattn_Wo': _L0_xattn_in['Wo'], 'L0_xattn_bo': _L0_xattn_in['bo'], 'L0_ffn_gate_w': _L0_ffn_in['gate_w'], 'L0_ffn_we_gate': _L0_ffn_in['we_gate'], 'L0_ffn_we_up': _L0_ffn_in['we_up'], 'L0_ffn_we_down': _L0_ffn_in['we_down'], 'L0_ffn_ws_gate': _L0_ffn_in['ws_gate'], 'L0_ffn_ws_up': _L0_ffn_in['ws_up'], 'L0_ffn_ws_down': _L0_ffn_in['ws_down'], 'L1_xattn_in_proj_w': _L1_xattn_in['in_proj_w'], 'L1_xattn_in_proj_b': _L1_xattn_in['in_proj_b'], 'L1_xattn_out_w': _L1_xattn_in['out_w'], 'L1_xattn_out_b': _L1_xattn_in['out_b'], 'L1_ffn_w1': _L1_ffn_in['w1'], 'L1_ffn_w2': _L1_ffn_in['w2'], 'L1_ffn_w3': _L1_ffn_in['w3'], 'L1_ffn_new_w1': _L1_ffn_in['new_w1'], 'L1_ffn_new_w2': _L1_ffn_in['new_w2'], 'L1_ffn_new_w3': _L1_ffn_in['new_w3'], 'L1_ffn_gate_weight': _L1_ffn_in['gate_weight'], 'L1_ffn_new_gate_weight': _L1_ffn_in['new_gate_weight'], 'L1_ffn_gate_bias': _L1_ffn_in['gate_bias'], 'L2_xattn_Wq_c': _L2_xattn_in['Wq_c'], 'L2_xattn_bq_c': _L2_xattn_in['bq_c'], 'L2_xattn_Wk_s': _L2_xattn_in['Wk_s'], 'L2_xattn_bk_s': _L2_xattn_in['bk_s'], 'L2_xattn_Wv_s': _L2_xattn_in['Wv_s'], 'L2_xattn_bv_s': _L2_xattn_in['bv_s'], 'L2_xattn_Wq_s': _L2_xattn_in['Wq_s'], 'L2_xattn_bq_s': _L2_xattn_in['bq_s'], 'L2_xattn_Wk_c': _L2_xattn_in['Wk_c'], 'L2_xattn_bk_c': _L2_xattn_in['bk_c'], 'L2_xattn_Wv_c': _L2_xattn_in['Wv_c'], 'L2_xattn_bv_c': _L2_xattn_in['bv_c'], 'L2_xattn_Wg': _L2_xattn_in['Wg'], 'L2_xattn_bg': _L2_xattn_in['bg'], 'L2_ffn_norm_weight': _L2_ffn_in['norm_weight'], 'L2_ffn_router_weight': _L2_ffn_in['router_weight'], 'L2_ffn_gate_up_weight': _L2_ffn_in['gate_up_weight'], 'L2_ffn_down_weight': _L2_ffn_in['down_weight'], 'L2_ffn_residual_alpha': _L2_ffn_in['residual_alpha'], 'L3_xattn_Wq': _L3_xattn_in['Wq'], 'L3_xattn_bq': _L3_xattn_in['bq'], 'L3_xattn_Wk': _L3_xattn_in['Wk'], 'L3_xattn_bk': _L3_xattn_in['bk'], 'L3_xattn_Wv': _L3_xattn_in['Wv'], 'L3_xattn_bv': _L3_xattn_in['bv'], 'L3_xattn_Wo': _L3_xattn_in['Wo'], 'L3_xattn_bo': _L3_xattn_in['bo'], 'L3_ffn_w_gate': _L3_ffn_in['w_gate'], 'L3_ffn_w_up': _L3_ffn_in['w_up'], 'L3_ffn_w_down': _L3_ffn_in['w_down']}

def reference(x, ctx_1024, mask_Bx1xSxS2_if1, mask_Bx1xS2_if1, g_xattn, g_ffn, L0_xattn_Wq, L0_xattn_Wk, L0_xattn_Wv, L0_xattn_Wo, L0_xattn_bo, L0_ffn_gate_w, L0_ffn_we_gate, L0_ffn_we_up, L0_ffn_we_down, L0_ffn_ws_gate, L0_ffn_ws_up, L0_ffn_ws_down, L1_xattn_in_proj_w, L1_xattn_in_proj_b, L1_xattn_out_w, L1_xattn_out_b, L1_ffn_w1, L1_ffn_w2, L1_ffn_w3, L1_ffn_new_w1, L1_ffn_new_w2, L1_ffn_new_w3, L1_ffn_gate_weight, L1_ffn_new_gate_weight, L1_ffn_gate_bias, L2_xattn_Wq_c, L2_xattn_bq_c, L2_xattn_Wk_s, L2_xattn_bk_s, L2_xattn_Wv_s, L2_xattn_bv_s, L2_xattn_Wq_s, L2_xattn_bq_s, L2_xattn_Wk_c, L2_xattn_bk_c, L2_xattn_Wv_c, L2_xattn_bv_c, L2_xattn_Wg, L2_xattn_bg, L2_ffn_norm_weight, L2_ffn_router_weight, L2_ffn_gate_up_weight, L2_ffn_down_weight, L2_ffn_residual_alpha, L3_xattn_Wq, L3_xattn_bq, L3_xattn_Wk, L3_xattn_bk, L3_xattn_Wv, L3_xattn_bv, L3_xattn_Wo, L3_xattn_bo, L3_ffn_w_gate, L3_ffn_w_up, L3_ffn_w_down):
    import jax
    import jax.numpy as jnp

    def _L0_xattn_ref(key, query, value, mask, Wq, Wk, Wv, Wo, bo):
        import jax, jax.numpy as jnp
        import numpy as np
        D_MODEL = 256
        HEADS = 16
        HEAD_DIM = D_MODEL // HEADS
        B, S = (2, 512)
        b, q_len, d = query.shape
        k_len = key.shape[1]
        h, hd = (HEADS, HEAD_DIM)
        q = (query @ Wq.T).reshape(b, q_len, h, hd)
        k = (key @ Wk.T).reshape(b, k_len, h, hd)
        v = (value @ Wv.T).reshape(b, k_len, h, hd)
        product = jnp.einsum('bqhd,bkhd->bhqk', q, k)
        product = jnp.where(mask == 0, jnp.float32(-1e+20), product)
        product = product / jnp.sqrt(jnp.asarray(hd, product.dtype))
        scores = jax.nn.softmax(product, axis=-1)
        out = jnp.einsum('bhqk,bkhd->bqhd', scores, v).reshape(b, q_len, h * hd)
        return out @ Wo.T + bo

    def _L0_ffn_ref(hidden_states, gate_w, we_gate, we_up, we_down, ws_gate, ws_up, ws_down):
        import math
        import jax, jax.numpy as jnp
        import numpy as np
        B, S, H = (4, 512, 256)
        E, K, I = (8, 2, 256)
        NSH = 2
        CF, RSF = (1.25, 1.0)
        orig_shape = hidden_states.shape
        x = hidden_states.reshape(-1, H)
        N = x.shape[0]
        logits = x.astype(jnp.float32) @ gate_w.astype(jnp.float32).T
        scores = jax.nn.softmax(logits, axis=-1)
        topk_w, topk_idx = jax.lax.top_k(scores, K)
        topk_w = topk_w / (topk_w.sum(-1, keepdims=True) + 1e-20) * RSF
        capacity = math.ceil(CF * N * K / E)
        flat = topk_idx.reshape(-1)
        one_hot = jax.nn.one_hot(flat, E, dtype=jnp.int32)
        pos = jnp.cumsum(one_hot, axis=0) - 1
        pos_tok = jnp.take_along_axis(pos, flat[:, None], axis=1)[:, 0]
        keep = (pos_tok < capacity).reshape(N, K)
        topk_w = topk_w * keep.astype(topk_w.dtype)
        comb = jnp.zeros((N, E), jnp.float32).at[jnp.arange(N)[:, None], topk_idx].add(topk_w)
        g = jnp.einsum('nh,eih->nei', x, we_gate)
        u = jnp.einsum('nh,eih->nei', x, we_up)
        eo = jnp.einsum('nei,ehi->neh', jax.nn.silu(g) * u, we_down)
        y = jnp.einsum('neh,ne->nh', eo, comb)
        sh = jax.nn.silu(x @ ws_gate.T) * (x @ ws_up.T) @ ws_down.T
        return (y + sh).reshape(orig_shape)

    def _L1_xattn_ref(q, k, v, in_proj_w, in_proj_b, out_w, out_b):
        import jax, jax.numpy as jnp
        import numpy as np
        B, S, E, H, W = (2, 1024, 256, 8, 8)

        def build_window_idx(seq_len):
            rows = []
            for t in range(seq_len):
                rp = [i for i in range(-4, 4) if 0 <= t + i < seq_len]
                while len(rp) < 8:
                    if t + len(rp) < seq_len:
                        rp.append(t + len(rp))
                    else:
                        rp.insert(0, t - (8 - len(rp)))
                rows.append([p % seq_len for p in rp])
            return np.asarray(rows, dtype=np.int32)
        b, s, e = q.shape
        d = e // H
        scale = 1.0 / np.sqrt(d).astype(np.float32)
        idx = jnp.asarray(build_window_idx(s))
        Wq, Wk, Wv = (in_proj_w[:e], in_proj_w[e:2 * e], in_proj_w[2 * e:])
        bq, bk, bv = (in_proj_b[:e], in_proj_b[e:2 * e], in_proj_b[2 * e:])
        kg = k[:, idx]
        vg = v[:, idx]
        qh = (q @ Wq.T + bq).reshape(b, s, H, d)
        kh = (kg @ Wk.T + bk).reshape(b, s, W, H, d)
        vh = (vg @ Wv.T + bv).reshape(b, s, W, H, d)
        scores = jnp.einsum('bshd,bswhd->bshw', qh * scale, kh)
        attn = jax.nn.softmax(scores, axis=-1)
        o = jnp.einsum('bshw,bswhd->bshd', attn, vh).reshape(b, s, e)
        return o @ out_w.T + out_b

    def _L1_ffn_ref(x, w1, w2, w3, new_w1, new_w2, new_w3, gate_weight, new_gate_weight, gate_bias):
        import jax, jax.numpy as jnp
        import numpy as np
        TOP_K = 2
        ROUTE_SCALE = 1.0
        EPS = 1e-20
        bs, slen, dim = x.shape
        x_flat = x.reshape(-1, dim)
        ew1 = jnp.concatenate([w1, new_w1], axis=0)
        ew2 = jnp.concatenate([w2, new_w2], axis=0)
        ew3 = jnp.concatenate([w3, new_w3], axis=0)
        gate = jnp.concatenate([gate_weight, new_gate_weight], axis=0)
        e_orig = w1.shape[0]
        e_tot = gate.shape[0]
        bias = jnp.concatenate([jnp.zeros((e_orig,), x.dtype), gate_bias])
        scores = jax.nn.sigmoid((x_flat @ gate.T + bias).astype(jnp.float32))
        top_scores, selected = jax.lax.top_k(scores, TOP_K)
        top_scores = top_scores / (jnp.sum(top_scores, axis=-1, keepdims=True) + EPS)
        top_scores = top_scores * ROUTE_SCALE
        onehot = jax.nn.one_hot(selected, e_tot, dtype=jnp.float32)
        cw = jnp.einsum('tk,tke->te', top_scores, onehot)
        out = jnp.zeros_like(x_flat)
        for e in range(e_tot):
            h = jax.nn.silu(x_flat @ ew1[e].T) * (x_flat @ ew3[e].T)
            out = out + cw[:, e:e + 1] * (h @ ew2[e].T)
        return out.reshape(bs, slen, dim)

    def _L2_xattn_ref(char_emb, subword_emb, Wq_c, bq_c, Wk_s, bk_s, Wv_s, bv_s, Wq_s, bq_s, Wk_c, bk_c, Wv_c, bv_c, Wg, bg):
        import jax, jax.numpy as jnp
        import numpy as np
        H = 256
        B = 8
        L_CHAR = 512
        L_SUB = 256

        def _linear(x, W, b):
            return jnp.einsum('blh,oh->blo', x, W) + b

        def _interp_linear(x, out_len):
            L_in = x.shape[1]
            pos = (jnp.arange(out_len, dtype=x.dtype) + 0.5) * (L_in / out_len) - 0.5
            pos = jnp.clip(pos, 0.0, L_in - 1)
            lo = jnp.floor(pos).astype(jnp.int32)
            hi = jnp.minimum(lo + 1, L_in - 1)
            w = (pos - lo.astype(x.dtype))[None, :, None]
            return x[:, lo] * (1 - w) + x[:, hi] * w
        h = char_emb.shape[-1]
        scale = 1.0 / jnp.sqrt(jnp.asarray(h, char_emb.dtype))
        Q_char = _linear(char_emb, Wq_c, bq_c)
        K_sub = _linear(subword_emb, Wk_s, bk_s)
        V_sub = _linear(subword_emb, Wv_s, bv_s)
        scores = jnp.einsum('bqh,bkh->bqk', Q_char, K_sub) * scale
        char2sub = jnp.einsum('bqk,bkh->bqh', jax.nn.softmax(scores, axis=-1), V_sub)
        Q_sub = _linear(subword_emb, Wq_s, bq_s)
        K_char = _linear(char_emb, Wk_c, bk_c)
        V_char = _linear(char_emb, Wv_c, bv_c)
        scores2 = jnp.einsum('bqh,bkh->bqk', Q_sub, K_char) * scale
        sub2char = jnp.einsum('bqk,bkh->bqh', jax.nn.softmax(scores2, axis=-1), V_char)
        L_char = char_emb.shape[1]
        if sub2char.shape[1] != L_char:
            sub2char = _interp_linear(sub2char, L_char)
        gate_in = jnp.concatenate([char2sub, sub2char], axis=-1)
        gate = jax.nn.sigmoid(jnp.einsum('blh,oh->blo', gate_in, Wg) + bg)
        return gate * char2sub + (1 - gate) * sub2char

    def _L2_ffn_ref(x, norm_weight, router_weight, gate_up_weight, down_weight, residual_alpha):
        import jax, jax.numpy as jnp
        import numpy as np
        DIM = 256
        HID = 704
        E = 8
        TOP_K = 2
        EPS = 1e-06

        def _rmsnorm(x, w):
            var = jnp.mean(jnp.square(x), axis=-1, keepdims=True)
            return x * jax.lax.rsqrt(var + EPS) * w
        normed = _rmsnorm(x, norm_weight)
        logits = jnp.einsum('bsd,ed->bse', normed, router_weight)
        probs = jax.nn.softmax(logits, axis=-1)
        topk_w, topk_idx = jax.lax.top_k(probs, TOP_K)
        topk_w = topk_w / jnp.sum(topk_w, axis=-1, keepdims=True)
        combine = jnp.sum(jax.nn.one_hot(topk_idx, E, dtype=normed.dtype) * topk_w[..., None], axis=-2)
        moe_out = jnp.zeros_like(x)
        for e in range(E):
            gu = jnp.einsum('bsd,hd->bsh', normed, gate_up_weight[e])
            gate, up = (gu[..., :HID], gu[..., HID:])
            hidden = jax.nn.silu(gate) * up
            out_e = jnp.einsum('bsh,dh->bsd', hidden, down_weight[e])
            moe_out = moe_out + combine[..., e, None] * out_e
        alpha = jnp.clip(residual_alpha, -0.5, 2.0)
        return x + alpha * moe_out

    def _L3_xattn_ref(query, key, value, mask, Wq, bq, Wk, bk, Wv, bv, Wo, bo):
        import jax, jax.numpy as jnp
        import numpy as np
        N_HEAD = 16
        N_FEAT = 256
        D_K = N_FEAT // N_HEAD
        B, Tq, F = query.shape
        Tk = key.shape[1]
        h, dk = (N_HEAD, D_K)
        q = (query @ Wq.T + bq).reshape(B, Tq, h, dk).transpose(0, 2, 1, 3)
        k = (key @ Wk.T + bk).reshape(B, Tk, h, dk).transpose(0, 2, 1, 3)
        v = (value @ Wv.T + bv).reshape(B, Tk, h, dk).transpose(0, 2, 1, 3)
        scale = 1.0 / np.sqrt(dk).astype(np.float32)
        scores = jnp.einsum('bhqd,bhkd->bhqk', q, k) * scale
        pad = mask[:, None, :, :] == 0
        min_value = jnp.finfo(scores.dtype).min
        scores = jnp.where(pad, min_value, scores)
        atten = jax.nn.softmax(scores, axis=-1)
        atten = jnp.where(pad, 0.0, atten)
        x = jnp.einsum('bhqk,bhkd->bhqd', atten, v)
        x = x.transpose(0, 2, 1, 3).reshape(B, Tq, h * dk)
        return x @ Wo.T + bo

    def _L3_ffn_ref(x, w_gate, w_up, w_down):
        import jax, jax.numpy as jnp
        import numpy as np
        DIM = 256
        HIDDEN = 768
        SCALE = 1.0 / 127.0

        def _dequant(w_int, dtype):
            return w_int.astype(dtype) * jnp.asarray(SCALE, dtype)
        wg = _dequant(w_gate, x.dtype)
        wu = _dequant(w_up, x.dtype)
        wd = _dequant(w_down, x.dtype)
        gate = jnp.einsum('bsd,hd->bsh', x, wg)
        up = jnp.einsum('bsd,hd->bsh', x, wu)
        h = jax.nn.silu(gate) * up
        return jnp.einsum('bsh,dh->bsd', h, wd)
    x = x + jnp.tanh(g_xattn[0]) * _L0_xattn_ref(ctx_1024, _layernorm(x, axis=-1), ctx_1024, mask_Bx1xSxS2_if1, L0_xattn_Wq, L0_xattn_Wk, L0_xattn_Wv, L0_xattn_Wo, L0_xattn_bo)
    x = x + jnp.tanh(g_ffn[0]) * _L0_ffn_ref(_layernorm(x, axis=-1), L0_ffn_gate_w, L0_ffn_we_gate, L0_ffn_we_up, L0_ffn_we_down, L0_ffn_ws_gate, L0_ffn_ws_up, L0_ffn_ws_down)
    x = x + jnp.tanh(g_xattn[1]) * _L1_xattn_ref(_layernorm(x, axis=-1), ctx_1024, ctx_1024, L1_xattn_in_proj_w, L1_xattn_in_proj_b, L1_xattn_out_w, L1_xattn_out_b)
    x = x + jnp.tanh(g_ffn[1]) * _L1_ffn_ref(_layernorm(x, axis=-1), L1_ffn_w1, L1_ffn_w2, L1_ffn_w3, L1_ffn_new_w1, L1_ffn_new_w2, L1_ffn_new_w3, L1_ffn_gate_weight, L1_ffn_new_gate_weight, L1_ffn_gate_bias)
    x = x + jnp.tanh(g_xattn[2]) * _L2_xattn_ref(_layernorm(x, axis=-1), ctx_1024, L2_xattn_Wq_c, L2_xattn_bq_c, L2_xattn_Wk_s, L2_xattn_bk_s, L2_xattn_Wv_s, L2_xattn_bv_s, L2_xattn_Wq_s, L2_xattn_bq_s, L2_xattn_Wk_c, L2_xattn_bk_c, L2_xattn_Wv_c, L2_xattn_bv_c, L2_xattn_Wg, L2_xattn_bg)
    x = x + jnp.tanh(g_ffn[2]) * _L2_ffn_ref(_layernorm(x, axis=-1), L2_ffn_norm_weight, L2_ffn_router_weight, L2_ffn_gate_up_weight, L2_ffn_down_weight, L2_ffn_residual_alpha)
    x = x + jnp.tanh(g_xattn[3]) * _L3_xattn_ref(_layernorm(x, axis=-1), ctx_1024, ctx_1024, mask_Bx1xS2_if1, L3_xattn_Wq, L3_xattn_bq, L3_xattn_Wk, L3_xattn_bk, L3_xattn_Wv, L3_xattn_bv, L3_xattn_Wo, L3_xattn_bo)
    x = x + jnp.tanh(g_ffn[3]) * _L3_ffn_ref(_layernorm(x, axis=-1), L3_ffn_w_gate, L3_ffn_w_up, L3_ffn_w_down)
    return x

_drawn_inputs = setup_inputs


def setup_inputs(seed=0):
    import zlib

    import numpy as np

    out = dict(_drawn_inputs(seed))
    spreads = {'L1_ffn_new_w2': (0.0, 0.379), 'L2_ffn_norm_weight': (1.0, 0.6)}
    factors = {'L0_xattn_Wq': 8.0,
     'L0_xattn_Wk': 8.0,
     'L0_xattn_bo': 3.153,
     'L0_ffn_gate_w': 6.92,
     'L0_ffn_we_gate': 6.436,
     'L0_ffn_we_up': 6.18,
     'L0_ffn_we_down': 6.27,
     'L0_ffn_ws_gate': 3.323,
     'L0_ffn_ws_up': 3.305,
     'L0_ffn_ws_down': 3.287,
     'L1_xattn_in_proj_b': 8.0,
     'L1_xattn_out_b': 2.883,
     'L1_ffn_w1': 3.617,
     'L1_ffn_w2': 3.45,
     'L1_ffn_w3': 3.419,
     'L2_xattn_Wq_c': 8.0,
     'L2_xattn_bq_c': 38.769,
     'L2_xattn_Wk_s': 8.0,
     'L2_xattn_bk_s': 64.0,
     'L2_xattn_bv_s': 8.0,
     'L2_xattn_Wq_s': 8.0,
     'L2_xattn_bq_s': 8.0,
     'L2_xattn_Wk_c': 8.0,
     'L2_xattn_bk_c': 64.0,
     'L2_xattn_Wv_c': 5.05,
     'L2_xattn_bv_c': 7.703,
     'L2_xattn_Wg': 8.0,
     'L2_xattn_bg': 37.465,
     'L2_ffn_router_weight': 8.0,
     'L2_ffn_gate_up_weight': 8.0,
     'L2_ffn_down_weight': 8.0,
     'L3_xattn_bq': 61.101,
     'L3_xattn_bk': 64.0,
     'L3_xattn_bv': 16.194,
     'L1_ffn_new_w1': 2.972,
     'L3_xattn_bo': 8.0}
    for name, (base, spread) in spreads.items():
        noise = np.random.default_rng([zlib.crc32(name.encode()), seed]).standard_normal(out[name].shape)
        drawn = base * np.exp(spread * noise) if base else spread * noise
        out[name] = jnp.asarray(drawn.astype(out[name].dtype))
    for name, factor in factors.items():
        out[name] = (out[name] * factor).astype(out[name].dtype)
    return out
```

```python
from contextlib import ExitStack

import concourse.bass as bass
from concourse import mybir

P = 128
F32 = mybir.dt.float32
F32R = mybir.dt.float32r
BF16 = mybir.dt.bfloat16
I32 = mybir.dt.int32
ALU = mybir.AluOpType
ACT = mybir.ActivationFunctionType
AX = mybir.AxisListType

B, S, D, SK = 4, 512, 256, 64
NT = B * S // P
TB = S // P
KC = D // P
LN_EPS = 1e-5

C_ID, C_TRI, C_ONE = 0, 128, 256
C_HB16 = 384
C_HB32 = 392
C_REV = 396
C_J = 405
C_WB = 445
C_CNT = 453
C_WBIAS = 501
C_INT = 549
NC = C_INT + 512


class Chain:

    def __init__(self, eng, sem):
        self.eng, self.sem, self.n = eng, sem, 0

    def add(self, ins):
        self.n += 1
        ins.then_inc(self.sem, 1)

    def wait(self):
        self.eng.wait_ge(self.sem, self.n)

    def link(self, ins):
        self.add(ins)
        self.wait()


class Core:

    def __init__(self, nc, ctx, ins, out):
        self.nc, self.ins, self.out, self.sems = nc, ins, out, []
        sb = lambda n, s, d=F32: ctx.enter_context(nc.sbuf_tensor(n, s, d))
        self.X = sb("X", [P, NT, D])
        self.XN = sb("XN", [P, NT, D])
        self.cst = sb("cst", [P, NC])
        self.idb = sb("idb", [P, P], BF16)
        self.tg = sb("tg", [P, 8])
        self.graw = sb("graw", [P, 8])
        self.ctxT = sb("ctxT", [P, KC, B * SK])
        self.ps = ctx.enter_context(nc.psum_tensor("ps", [P, 8, 512], F32))
        self.ident = self.cst[:, C_ID:C_ID + P]
        self.xs_dram = nc.dram_tensor("sorted_rows", (44 * P, D), F32).ap()
        self.y_dram = nc.dram_tensor("expert_rows", (44 * P, D), F32).ap()


    def sem(self, name):
        self.sems.append(self.nc.alloc_semaphore(name=name))
        return self.sems[-1]

    def clear(self):
        self.nc.clear_and_free_semaphores(self.sems)
        self.nc.all_engine_barrier()
        self.sems = []


class Norm:

    def __init__(self, k, sb, sem, name, split, reuse=False):
        self.k, self.split, self.reuse = k, split, reuse
        self.st = sb(name + "_stats", [P, TB, 6])
        self.mv = sb(name + "_mv", [P, TB, 2])
        self.v = sb(name + "_v", [P, 5, TB])
        self.normed = sem(name + "_normed")
        self.step = sem(name + "_norm_step")
        self.xt_ready = sem(name + "_xt_ready")
        self.xh_done = sem(name + "_xh_done")
        self.xl_done = sem(name + "_xl_done")
        if split:
            self.xh = sb(name + "_xh", [P, 2, KC, S], F32R)
            self.xl = sb(name + "_xl", [P, 2, KC, S], F32R)
        else:
            self.xf = sb(name + "_xf", [P, 2, KC, S])
        self.chain = None

    def rsqrt(self, dve, v, y, t, hv, ti):
        nc, ch = self.k.nc, self.chain
        ch.add(nc.vector.tensor_scalar(hv, v, -0.5, None, ALU.mult))
        ch.link(nc.vector.tensor_scalar(ti, v.bitcast(I32), 1, None, ALU.logical_shift_right))
        ch.link(nc.vector.tensor_scalar(y.bitcast(I32), ti, -1.0, float(0x5F3759DF), ALU.mult, ALU.add))
        for _ in range(3):
            ch.link(nc.vector.tensor_tensor(t, y, y, ALU.mult))
            ch.link(nc.vector.tensor_tensor(t, t, hv, ALU.mult))
            ch.link(nc.vector.scalar_tensor_tensor(y, t, 1.5, y, ALU.add, ALU.mult))

    def dve_norm(self, dve, b):
        nc, k = self.k.nc, self.k
        if self.chain is None:
            self.chain = Chain(dve, self.step)
        ch = self.chain
        for i in range(TB):
            ch.add(nc.vector.bn_stats(self.st[:, i, :], k.X[:, b * TB + i, :]))
        ch.wait()
        for i in range(TB):
            ch.add(nc.vector.bn_aggr(self.mv[:, i, :], self.st[:, i, :]))
        ch.wait()
        v = self.v
        ch.link(nc.vector.tensor_scalar(v[:, 0, :], self.mv[:, :, 1], LN_EPS, None, ALU.add))
        self.rsqrt(dve, v[:, 0, :], v[:, 1, :], v[:, 2, :], v[:, 3, :], v[:, 4, :].bitcast(I32))
        for i in range(TB):
            t = b * TB + i
            nc.vector.tensor_scalar(k.XN[:, t, :], k.X[:, t, :], self.mv[:, i, 0:1], v[:, 1, i:i + 1],
                                    ALU.subtract, ALU.mult).then_inc(self.normed, 1)

    def pe_transpose(self, pe, b, bank):
        nc, k = self.k.nc, self.k
        if not self.reuse:
            pe.wait_ge(self.normed, TB * (b + 1))
        for c in range(KC):
            for i in range(TB):
                last = nc.tensor.transpose(k.ps[:, bank + c, i * P:(i + 1) * P],
                                           k.XN[:, b * TB + i, c * P:(c + 1) * P], k.ident)
        last.then_inc(self.xt_ready, 1)

    def act_evacuate(self, act, b, bank):
        nc, k = self.k.nc, self.k
        act.wait_ge(self.xt_ready, b + 1)
        dst = (self.xh if self.split else self.xf)[:, b % 2]
        nc.scalar.activation(dst, k.ps[:, bank:bank + KC, :], ACT.Copy).then_inc(self.xh_done, 1)

    def dve_low(self, dve, b, bank):
        nc, k = self.k.nc, self.k
        dve.wait_ge(self.xh_done, b + 1)
        nc.vector.tensor_tensor(self.xl[:, b % 2], k.ps[:, bank:bank + KC, :],
                                self.xh[:, b % 2].bitcast(F32), ALU.subtract).then_inc(self.xl_done, 1)


def matmul3(nc, out, lh, ll, rh, rl, start, stop):
    nc.tensor.matmul(out, ll, rh, start=start, stop=False)
    nc.tensor.matmul(out, lh, rl, start=False, stop=False)
    return nc.tensor.matmul(out, lh, rh, start=False, stop=stop)


def prologue(k):
    nc = k.nc
    with ExitStack() as ctx:
        loaded = k.sem("pro_loaded")
        zeroed = k.sem("pro_zeroed")
        cleared = k.sem("pro_cleared")
        zero = ctx.enter_context(nc.sbuf_tensor("pro_zero", [P, 1024], F32))
        block = ctx.enter_context(nc.Block())

        @block.sync
        def _(sp):
            sp.dma_start(k.X[:], k.ins["x"].rearrange("(t p) d -> p t d", p=P)).then_inc(loaded, 16)
            sp.dma_start(k.cst[:], k.ins["cst"]).then_inc(loaded, 16)
            sp.dma_start(k.ctxT[:], k.ins["ctxT"]).then_inc(loaded, 16)
            sp.dma_start(k.graw[:, 0:4], k.ins["g_xattn"].unsqueeze(0).to_broadcast([P, 4])).then_inc(loaded, 16)
            sp.dma_start(k.graw[:, 4:8], k.ins["g_ffn"].unsqueeze(0).to_broadcast([P, 4])).then_inc(loaded, 16)
            sp.wait_ge(loaded, 80)
            sp.wait_ge(zeroed, 1)
            rows = k.xs_dram.rearrange("(n p r) d -> n p (r d)", p=P, r=4)
            for n in range(rows.shape[0]):
                sp.dma_start(rows[n], zero[:]).then_inc(cleared, 16)
            sp.wait_ge(cleared, 16 * rows.shape[0])

        @block.scalar
        def _(act):
            act.wait_ge(loaded, 80)
            nc.scalar.activation(k.tg[:], k.graw[:], ACT.Tanh)

        @block.vector
        def _(dve):
            nc.vector.memset(zero[:], 0.0).then_inc(zeroed, 1)
            dve.wait_ge(loaded, 80)
            nc.vector.tensor_copy(k.idb[:], k.ident)


def attention16(k, layer):
    nc, ps = k.nc, k.ps
    biased = layer == 3
    tag = f"a{layer}"
    gate = k.tg[:, layer:layer + 1]
    with ExitStack() as ctx:
        sb = lambda n, s, d=F32: ctx.enter_context(nc.sbuf_tensor(f"{tag}_{n}", s, d))
        sem = lambda n: k.sem(f"{tag}_{n}")
        norm = Norm(k, sb, sem, "n", True)
        W = sb("w", [P, 4, KC, D])
        wqh, wql = sb("wqh", [P, KC, D], F32R), sb("wql", [P, KC, D], F32R)
        woh, wol = sb("woh", [P, KC, D], F32R), sb("wol", [P, KC, D], F32R)
        ctx2 = sb("ctx2", [P, KC, B, 2, SK])
        kT = sb("kT", [P, KC, B * SK])
        kbd = sb("kbd", [P, KC, B, 8, SK])
        vbd = sb("vbd", [P, B, 8, 34])
        qT = sb("qT", [P, 2, KC, S])
        E = sb("e", [P, 2, 16, SK])
        mx = sb("mx", [P, 2, 16])
        pt = sb("pt", [P, 2, 8, P])
        rs = sb("rs", [P, 8, 2])
        on = sb("on", [P, 2, D])
        oth, otl = sb("oth", [P, 2, KC, P], F32R), sb("otl", [P, 2, KC, P], F32R)
        brow = sb("brow", [P, D])
        bqk = sb("bqk", [P, 2, KC])
        bv = sb("bv", [1, D])
        if biased:
            mraw = sb("mraw", [1, B * SK], I32)
            mb = sb("mb", [1, B, SK], BF16)
            kraw = sb("kraw", [P, B], I32)
            keep = sb("keep", [P, B])
            onesb = sb("onesb", [1, P], BF16)
        else:
            mraw = sb("mraw", [P, NT, SK], I32)
            mb = sb("mb", [P, NT, SK], BF16)

        loaded, dstep = sem("loaded"), sem("dve_step")
        whi, ctx2_done = sem("weights_hi"), sem("ctx2_done")
        k_ready, k_copied, kbd_done = sem("k_ready"), sem("k_copied"), sem("kbd_done")
        v_ready, v_done = sem("v_ready"), sem("v_done")
        wl_done = sem("weights_lo")
        q_ready, q_done = sem("q_ready"), sem("q_done")
        s_ready, sub_done, exp_done = sem("s_ready"), sem("sub_done"), sem("exp_done")
        pt_ready, pt_done = sem("pt_ready"), sem("pt_done")
        o_ready, on_done, ot_ready = sem("o_ready"), sem("on_done"), sem("ot_ready")
        oth_done, otl_done, y_ready, y_done = sem("oth_done"), sem("otl_done"), sem("y_ready"), sem("y_done")
        bias_scaled, bias_added = sem("bias_scaled"), sem("bias_added")
        BT, BS, BP, BO = 0, 2, 4, 6
        n_loads = 6 if biased else 3
        block = ctx.enter_context(nc.Block())

        @block.sync
        def _(sp):
            sp.dma_start(W[:], k.ins[f"w_{tag}"]).then_inc(loaded, 16)
            sp.dma_start(brow[:], k.ins[f"bo_{tag}"].unsqueeze(0).to_broadcast([P, D])).then_inc(loaded, 16)
            if biased:
                sp.dma_start(bqk[:], k.ins[f"bqk_{tag}"]).then_inc(loaded, 16)
                sp.dma_start(bv[:], k.ins[f"bv_{tag}"].unsqueeze(0)).then_inc(loaded, 16)
                sp.dma_start(mraw[:], k.ins["mask_k"].rearrange("b k -> (b k)").unsqueeze(0)).then_inc(loaded, 16)
                with nc.allow_non_contiguous_dma("a small mask, by key"):
                    for h in range(2):
                        sp.dma_start(kraw[h * SK:(h + 1) * SK, :],
                                     k.ins["mask_k"].rearrange("b k -> k b")).then_inc(loaded, 8 * 2)
            else:
                sp.dma_start(mraw[:], k.ins["mask_q"].rearrange("(t p) k -> p t k", p=P)).then_inc(loaded, 16)
            sp.wait_ge(loaded, 16 * (n_loads + biased))

        @block.gpsimd
        def _(pool):
            pool.wait_ge(loaded, 16 * (n_loads + biased))
            nc.gpsimd.tensor_scalar(brow[:], brow[:], gate, 0.0, ALU.mult, ALU.add).then_inc(bias_scaled, 1)
            pool.wait_ge(bias_scaled, 1)
            for t in range(NT):
                pool.wait_ge(norm.normed, t + 1)
                nc.gpsimd.tensor_tensor(k.X[:, t, :], k.X[:, t, :], brow[:], ALU.add).then_inc(bias_added, 1)

        @block.scalar
        def _(act):
            act.wait_ge(loaded, 16 * (n_loads + biased))
            nc.scalar.activation(wqh[:], W[:, 0], ACT.Copy).then_inc(whi, 1)
            nc.scalar.activation(woh[:], W[:, 3], ACT.Copy).then_inc(whi, 1)
            act.wait_ge(k_ready, 1)
            for c in range(KC):
                if biased:
                    nc.scalar.activation(kT[:, c], ps[:, BS + c, 0:B * SK], ACT.Identity,
                                         bias=bqk[:, 1, c:c + 1]).then_inc(k_copied, 1)
                else:
                    nc.scalar.activation(kT[:, c], ps[:, BS + c, 0:B * SK], ACT.Copy).then_inc(k_copied, 1)

            def queries(b):
                act.wait_ge(q_ready, b + 1)
                for c in range(KC):
                    if biased:
                        nc.scalar.activation(qT[:, b % 2, c], ps[:, BT + c, :], ACT.Identity,
                                             bias=bqk[:, 0, c:c + 1]).then_inc(q_done, 1)
                    else:
                        nc.scalar.activation(qT[:, b % 2, c], ps[:, BT + c, :], ACT.Copy).then_inc(q_done, 1)

            norm.act_evacuate(act, 0, BT)
            queries(0)
            for i in range(NT + 2):
                if 2 <= i:
                    u = i - 2
                    act.wait_ge(ot_ready, u + 1)
                    nc.scalar.activation(oth[:, u % 2], ps[:, BO + u % 2, 0:D].rearrange("p (c q) -> p c q", c=KC),
                                         ACT.Copy).then_inc(oth_done, 1)
                if 1 <= i <= NT:
                    u = i - 1
                    act.wait_ge(pt_ready, u + 1)
                    nc.scalar.activation(pt[:, u % 2], ps[:, BP:BP + 2, :].rearrange("p a (j q) -> p (a j) q", j=4),
                                         ACT.Copy).then_inc(pt_done, 1)
                if i < NT:
                    act.wait_ge(sub_done, i + 1)
                    nc.scalar.activation(E[:, i % 2], E[:, i % 2], ACT.Exp, scale=0.25).then_inc(exp_done, 1)
                    b = i // TB + 1
                    if i % TB == 1 and b < B:
                        norm.act_evacuate(act, b, BT)
                    if i % TB == 2 and b < B:
                        queries(b)

        @block.vector
        def _(dve):
            ch = Chain(dve, dstep)
            nc.vector.tensor_copy(ctx2[:], k.ctxT[:].rearrange("p c (b s) -> p c b s", b=B).unsqueeze(3)
                                  .to_broadcast([P, KC, B, 2, SK])).then_inc(ctx2_done, 1)
            norm.dve_norm(dve, 0)
            ch.link(nc.vector.memset(vbd[:], 0.0))
            ch.add(nc.vector.memset(vbd[0:64, :, :, 16:17], 1.0))
            ch.add(nc.vector.memset(vbd[64:128, :, :, 33:34], 1.0))
            dve.wait_ge(loaded, 16 * (n_loads + biased))
            if biased:
                ch.add(nc.vector.memset(onesb[:], 1.0))
                ch.add(nc.vector.tensor_scalar(keep[:], kraw[:], 0, None, ALU.not_equal))
                ch.add(nc.vector.tensor_scalar(mb[:], mraw[:].rearrange("o (b s) -> o b s", b=B), 0, -1e38,
                                               ALU.is_equal, ALU.mult))
            else:
                ch.add(nc.vector.tensor_scalar(mb[:], mraw[:], 0, -1e20, ALU.is_equal, ALU.mult))
            ch.wait()
            dve.wait_ge(whi, 1)
            nc.vector.tensor_tensor(wql[:], W[:, 0], wqh[:].bitcast(F32), ALU.subtract).then_inc(wl_done, 1)
            dve.wait_ge(whi, 2)
            nc.vector.tensor_tensor(wol[:], W[:, 3], woh[:].bitcast(F32), ALU.subtract).then_inc(wl_done, 1)
            norm.dve_low(dve, 0, BT)
            for c in range(KC):
                dve.wait_ge(k_copied, c + 1)
                nc.vector.tensor_tensor(
                    kbd[:, c], kT[:, c].rearrange("p (b s) -> p b s", b=B).unsqueeze(2).to_broadcast([P, B, 8, SK]),
                    k.cst[:, C_HB16:C_HB16 + 8].unsqueeze(1).unsqueeze(3).to_broadcast([P, B, 8, SK]),
                    ALU.mult).then_inc(kbd_done, 1)
            for b in range(B):
                dve.wait_ge(v_ready, b + 1)
                for h in range(2):
                    src = ps[h * 64:h * 64 + 64, BP + b % 2, 0:D].rearrange("p (j h d) -> p j h d", h=2, d=16)[:, :, h]
                    dst = vbd[h * 64:h * 64 + 64, b, :, 17 * h:17 * h + 16]
                    if biased:
                        nc.vector.tensor_scalar(dst, src, keep[h * 64:h * 64 + 64, b:b + 1], None,
                                                ALU.mult).then_inc(v_done, 1)
                    else:
                        nc.vector.tensor_copy(dst, src).then_inc(v_done, 1)
            for i in range(NT + 2):
                if i < NT:
                    dve.wait_ge(s_ready, i + 1)
                    sc = ps[:, BS:BS + 2, :].rearrange("p a (h s) -> p (a h) s", s=SK)
                    ch.link(nc.vector.tensor_reduce(mx[:, i % 2], sc, AX.X, ALU.max))
                    nc.vector.tensor_tensor(E[:, i % 2], sc, mx[:, i % 2].unsqueeze(2).to_broadcast([P, 16, SK]),
                                            ALU.subtract).then_inc(sub_done, 1)
                    b = i // TB + 1
                    if i % TB == 0 and b < B:
                        norm.dve_norm(dve, b)
                    if i % TB == 1 and b < B:
                        norm.dve_low(dve, b, BT)
                if 2 <= i:
                    u = i - 2
                    dve.wait_ge(oth_done, u + 1)
                    nc.vector.tensor_tensor(otl[:, u % 2], ps[:, BO + u % 2, 0:D].rearrange("p (c q) -> p c q", c=KC),
                                            oth[:, u % 2].bitcast(F32), ALU.subtract).then_inc(otl_done, 1)
                    dve.wait_ge(y_ready, u + 1)
                    dve.wait_ge(bias_added, u + 1)
                    nc.vector.scalar_tensor_tensor(k.X[:, u, :], ps[:, BO + u % 2, D:2 * D], gate, k.X[:, u, :],
                                                   ALU.mult, ALU.add).then_inc(y_done, 1)
                if 1 <= i <= NT:
                    u = i - 1
                    dve.wait_ge(o_ready, u + 1)
                    o = ps[:, BO + u % 2, 0:272].rearrange("p (j h d) -> p j h d", h=2, d=17)
                    ch.link(nc.vector.reciprocal(rs[:], o[:, :, :, 16]))
                    nc.vector.tensor_tensor(on[:, u % 2].rearrange("p (j h d) -> p j h d", h=2, d=16),
                                            o[:, :, :, 0:16], rs[:].unsqueeze(3).to_broadcast([P, 8, 2, 16]),
                                            ALU.mult).then_inc(on_done, 1)

        @block.tensor
        def _(pe):
            pe.wait_ge(loaded, 16 * (n_loads + biased))
            for c in range(KC):
                for j in range(KC):
                    last = nc.tensor.matmul(ps[:, BS + c, 0:B * SK], W[:, 1, j, c * P:(c + 1) * P], k.ctxT[:, j, :],
                                            start=(j == 0), stop=(j == KC - 1))
            last.then_inc(k_ready, 1)
            norm.pe_transpose(pe, 0, BT)
            pe.wait_ge(ctx2_done, 1)
            for b in range(B):
                if b >= 2:
                    pe.wait_ge(v_done, 2 * (b - 1))
                for j in range(KC):
                    last = nc.tensor.matmul(ps[:, BP + b % 2, 0:D], ctx2[:, j, b].rearrange("p a s -> p (a s)"),
                                            W[:, 2, j, :], start=(j == 0), stop=(j == KC - 1 and not biased))
                if biased:
                    last = nc.tensor.matmul(ps[:, BP + b % 2, 0:D], k.cst[0:1, C_ONE:C_ONE + P], bv[:],
                                            start=False, stop=True)
                last.then_inc(v_ready, 1)

            def queries(b):
                pe.wait_ge(norm.xl_done, b + 1)
                if b == 0:
                    pe.wait_ge(wl_done, 1)
                for c in range(KC):
                    for j in range(KC):
                        last = matmul3(nc, ps[:, BT + c, :], wqh[:, j, c * P:(c + 1) * P], wql[:, j, c * P:(c + 1) * P],
                                       norm.xh[:, b % 2, j], norm.xl[:, b % 2, j], j == 0, j == KC - 1)
                last.then_inc(q_ready, 1)

            def scores(t):
                b = t // TB
                pe.wait_ge(q_done, KC * (b + 1))
                if t == 0:
                    pe.wait_ge(kbd_done, 2)
                    pe.wait_ge(dstep, 4 if not biased else 6)
                else:
                    pe.wait_ge(sub_done, t)
                for c in range(KC):
                    if biased:
                        mask = mb[:, b, :].unsqueeze(1).to_broadcast([1, 8, SK])
                        lhs = onesb[:]
                    else:
                        mask = mb[:, t, :].unsqueeze(1).to_broadcast([P, 8, SK])
                        lhs = k.idb[:]
                    nc.tensor.matmul(ps[:, BS + c, :].rearrange("p (h s) -> p h s", s=SK), lhs, mask, start=True, stop=False)
                    last = nc.tensor.matmul(ps[:, BS + c, :], qT[:, b % 2, c, (t % TB) * P:(t % TB + 1) * P],
                                            kbd[:, c, b].rearrange("p h s -> p (h s)"), start=False, stop=True)
                last.then_inc(s_ready, 1)

            queries(0)
            for i in range(NT + 2):
                if i < NT:
                    scores(i)
                if 2 <= i:
                    u = i - 2
                    pe.wait_ge(on_done, u + 1)
                    for c in range(KC):
                        last = nc.tensor.transpose(ps[:, BO + u % 2, c * P:(c + 1) * P], on[:, u % 2, c * P:(c + 1) * P],
                                                   k.ident)
                    last.then_inc(ot_ready, 1)
                if 1 <= i <= NT:
                    u = i - 1
                    pe.wait_ge(exp_done, u + 1)
                    if u >= 1:
                        pe.wait_ge(pt_done, u)
                    else:
                        pe.wait_ge(v_done, 2 * B)
                    for j in range(8):
                        last = nc.tensor.transpose(ps[:, BP + j // 4, (j % 4) * P:(j % 4 + 1) * P],
                                                   E[:, u % 2, 2 * j:2 * j + 2, :].rearrange("p h s -> p (h s)"),
                                                   k.ident)
                    last.then_inc(pt_ready, 1)
                if 2 <= i:
                    u = i - 2
                    pe.wait_ge(otl_done, u + 1)
                    if u == 0:
                        pe.wait_ge(wl_done, 2)
                    for j in range(KC):
                        last = matmul3(nc, ps[:, BO + u % 2, D:2 * D], oth[:, u % 2, j], otl[:, u % 2, j],
                                       woh[:, j], wol[:, j], j == 0, j == KC - 1)
                    last.then_inc(y_ready, 1)
                if 1 <= i <= NT:
                    u = i - 1
                    pe.wait_ge(pt_done, u + 1)
                    if u >= 2:
                        pe.wait_ge(y_done, u - 1)
                    for j in range(8):
                        last = nc.tensor.matmul(ps[:, BO + u % 2, 34 * j:34 * j + 34], pt[:, u % 2, j],
                                                vbd[:, u // TB, j, :], start=True, stop=True)
                    last.then_inc(o_ready, 1)
                if i < NT:
                    b = i // TB + 1
                    if i % TB == 0 and b < B:
                        pe.wait_ge(q_done, KC * b)
                        norm.pe_transpose(pe, b, BT)
                    if i % TB == 1 and b < B:
                        queries(b)


def window_attention(k):
    nc, ps = k.nc, k.ps
    H, HD, WK = 8, 32, 12
    HW = H * WK
    gate = k.tg[:, 1:2]
    with ExitStack() as ctx:
        sb = lambda n, s, d=F32: ctx.enter_context(nc.sbuf_tensor(f"a1_{n}", s, d))
        sem = lambda n: k.sem(f"a1_{n}")
        norm = Norm(k, sb, sem, "n", True)
        W = sb("w", [P, 4, KC, D])
        wqh, wql = sb("wqh", [P, KC, D], F32R), sb("wql", [P, KC, D], F32R)
        woh, wol = sb("woh", [P, KC, D], F32R), sb("wol", [P, KC, D], F32R)
        ctxw = sb("ctxw", [P, KC, B, H, WK])
        kT = sb("kT", [P, KC, B, WK])
        kbd = sb("kbd", [P, KC, B, 4, WK])
        vbd = sb("vbd", [HW, B, H, HD])
        qT = sb("qT", [P, 2, KC, S])
        E = sb("e", [P, 2, TB * H, WK])
        mx, rs = sb("mx", [P, TB * H]), sb("rs", [P, TB * H])
        pT = sb("pT", [HW, 2, S])
        oth, otl = sb("oth", [P, 2, KC, S], F32R), sb("otl", [P, 2, KC, S], F32R)
        brow = sb("brow", [P, D])
        bqk = sb("bqk", [P, 2, KC])
        bv = sb("bv", [1, D])

        loaded, dstep = sem("loaded"), sem("dve_step")
        whi, wl_done, ctxw_done = sem("weights_hi"), sem("weights_lo"), sem("ctxw_done")
        k_ready, k_copied, kbd_done = sem("k_ready"), sem("k_copied"), sem("kbd_done")
        v_ready, v_done = sem("v_ready"), sem("v_done")
        q_ready, q_done, s_ready, s_read = sem("q_ready"), sem("q_done"), sem("s_ready"), sem("s_read")
        sub_done, exp_done, p_done = sem("sub_done"), sem("exp_done"), sem("p_done")
        pt_ready, pt_done, ot_ready = sem("pt_ready"), sem("pt_done"), sem("ot_ready")
        oth_done, otl_done, y_ready, y_done = sem("oth_done"), sem("otl_done"), sem("y_ready"), sem("y_done")
        bias_scaled, bias_added = sem("bias_scaled"), sem("bias_added")
        BT, BS, BP, BY, BO = 0, 2, 3, 4, 6

        block = ctx.enter_context(nc.Block())

        @block.sync
        def _(sp):
            sp.dma_start(W[:], k.ins["w_a1"]).then_inc(loaded, 16)
            sp.dma_start(brow[:], k.ins["bo_a1"].unsqueeze(0).to_broadcast([P, D])).then_inc(loaded, 16)
            sp.dma_start(bqk[:], k.ins["bqk_a1"]).then_inc(loaded, 16)
            sp.dma_start(bv[:], k.ins["bv_a1"].unsqueeze(0)).then_inc(loaded, 16)
            sp.wait_ge(loaded, 64)

        @block.gpsimd
        def _(pool):
            pool.wait_ge(loaded, 64)
            nc.gpsimd.tensor_scalar(brow[:], brow[:], gate, 0.0, ALU.mult, ALU.add).then_inc(bias_scaled, 1)
            pool.wait_ge(bias_scaled, 1)
            for t in range(NT):
                pool.wait_ge(norm.normed, t + 1)
                nc.gpsimd.tensor_tensor(k.X[:, t, :], k.X[:, t, :], brow[:], ALU.add).then_inc(bias_added, 1)

        @block.scalar
        def _(act):
            act.wait_ge(loaded, 64)
            nc.scalar.activation(wqh[:], W[:, 0], ACT.Copy).then_inc(whi, 1)
            nc.scalar.activation(woh[:], W[:, 3], ACT.Copy).then_inc(whi, 1)
            act.wait_ge(k_ready, 1)
            for c in range(KC):
                nc.scalar.activation(kT[:, c], ps[:, BY + c, 0:B * WK].rearrange("p (b s) -> p b s", b=B),
                                     ACT.Identity, bias=bqk[:, 1, c:c + 1]).then_inc(k_copied, 1)

            def queries(b):
                norm.act_evacuate(act, b, BT)
                act.wait_ge(q_ready, b + 1)
                for c in range(KC):
                    nc.scalar.activation(qT[:, b % 2, c], ps[:, BT + c, :], ACT.Identity,
                                         bias=bqk[:, 0, c:c + 1]).then_inc(q_done, 1)

            queries(0)
            for b in range(B):
                act.wait_ge(sub_done, b + 1)
                nc.scalar.activation(E[:, b % 2], E[:, b % 2], ACT.Exp, scale=HD ** -0.5).then_inc(exp_done, 1)
                if b + 1 < B:
                    queries(b + 1)
                act.wait_ge(pt_ready, b + 1)
                nc.scalar.activation(pT[:, b % 2], ps[0:HW, BP, :], ACT.Copy).then_inc(pt_done, 1)
                act.wait_ge(ot_ready, b + 1)
                nc.scalar.activation(oth[:, b % 2], ps[:, BO:BO + KC, :], ACT.Copy).then_inc(oth_done, 1)

        @block.vector
        def _(dve):
            ch = Chain(dve, dstep)
            ctx4 = k.ctxT[:].rearrange("p c (b s) -> p c b s", b=B)
            for c in range(KC):
                for b in range(B):
                    ch.add(nc.vector.tensor_copy(ctxw[:, c, b, :, 0:WK - 1],
                                                 ctx4[:, c, b, 0:WK - 1].unsqueeze(1).to_broadcast([P, H, WK - 1])))
            nc.vector.tensor_copy(ctxw[:, :, :, :, WK - 1], ctx4[:, :, :, SK - 1].unsqueeze(3)
                                  .to_broadcast([P, KC, B, H])).then_inc(ctxw_done, 1)
            norm.dve_norm(dve, 0)
            dve.wait_ge(whi, 1)
            nc.vector.tensor_tensor(wql[:], W[:, 0], wqh[:].bitcast(F32), ALU.subtract).then_inc(wl_done, 1)
            dve.wait_ge(whi, 2)
            nc.vector.tensor_tensor(wol[:], W[:, 3], woh[:].bitcast(F32), ALU.subtract).then_inc(wl_done, 1)
            norm.dve_low(dve, 0, BT)
            for c in range(KC):
                dve.wait_ge(k_copied, c + 1)
                nc.vector.tensor_tensor(kbd[:, c], kT[:, c].unsqueeze(2).to_broadcast([P, B, 4, WK]),
                                        k.cst[:, C_HB32:C_HB32 + 4].unsqueeze(1).unsqueeze(3).to_broadcast([P, B, 4, WK]),
                                        ALU.mult).then_inc(kbd_done, 1)
            for b in range(B):
                dve.wait_ge(v_ready, b + 1)
                nc.vector.tensor_tensor(vbd[:, b], ps[0:HW, BP + 3 * (b % 2), 0:D].rearrange("p (h d) -> p h d", h=H),
                                        k.cst[0:HW, C_WB:C_WB + H].unsqueeze(2).to_broadcast([HW, H, HD]),
                                        ALU.mult).then_inc(v_done, 1)
            norm.dve_norm(dve, 1)
            cnt = k.cst[:, C_CNT:C_CNT + 48].rearrange("p (t s) -> p t s", t=TB).unsqueeze(2).to_broadcast([P, TB, H, WK])
            off = k.cst[:, C_WBIAS:C_WBIAS + 48].rearrange("p (t s) -> p t s", t=TB).unsqueeze(2) \
                .to_broadcast([P, TB, H, WK])
            for b in range(B):
                dve.wait_ge(s_ready, b + 1)
                e = E[:, b % 2]
                e4 = e.rearrange("p (t h) s -> p t h s", t=TB)
                nc.vector.tensor_tensor(e4, ps[:, BS, 0:TB * HW].rearrange("p (t h s) -> p t h s", t=TB, h=H), off,
                                        ALU.add).then_inc(s_read, 1)
                dve.wait_ge(s_read, b + 1)
                ch.link(nc.vector.tensor_reduce(mx[:], e, AX.X, ALU.max))
                nc.vector.tensor_tensor(e, e, mx[:].unsqueeze(2).to_broadcast([P, TB * H, WK]),
                                        ALU.subtract).then_inc(sub_done, 1)
                if b + 1 < B:
                    norm.dve_low(dve, b + 1, BT)
                dve.wait_ge(exp_done, b + 1)
                ch.link(nc.vector.tensor_tensor(e4, e4, cnt, ALU.mult))
                ch.link(nc.vector.tensor_reduce(rs[:], e, AX.X, ALU.add))
                ch.link(nc.vector.reciprocal(rs[:], rs[:]))
                nc.vector.tensor_tensor(e, e, rs[:].unsqueeze(2).to_broadcast([P, TB * H, WK]),
                                        ALU.mult).then_inc(p_done, 1)
                if b + 2 < B:
                    norm.dve_norm(dve, b + 2)
                dve.wait_ge(oth_done, b + 1)
                nc.vector.tensor_tensor(otl[:, b % 2], ps[:, BO:BO + KC, :], oth[:, b % 2].bitcast(F32),
                                        ALU.subtract).then_inc(otl_done, 1)
                dve.wait_ge(y_ready, b + 1)
                dve.wait_ge(bias_added, TB * (b + 1))
                xb = k.X[:, b * TB:(b + 1) * TB, :]
                nc.vector.scalar_tensor_tensor(xb, ps[:, BY:BY + 2, :].rearrange("p a (t d) -> p (a t) d", t=2), gate, xb,
                                               ALU.mult, ALU.add).then_inc(y_done, 1)

        @block.tensor
        def _(pe):
            pe.wait_ge(loaded, 64)
            pe.wait_ge(ctxw_done, 1)
            for c in range(KC):
                for j in range(KC):
                    last = nc.tensor.matmul(ps[:, BY + c, 0:B * WK].rearrange("p (b s) -> p b s", b=B),
                                            W[:, 1, j, c * P:(c + 1) * P], ctxw[:, j, :, 0, :],
                                            start=(j == 0), stop=(j == KC - 1))
            last.then_inc(k_ready, 1)
            norm.pe_transpose(pe, 0, BT)
            for b in range(B):
                if b >= 2:
                    pe.wait_ge(v_done, b - 1)
                out = ps[0:HW, BP + 3 * (b % 2), 0:D]
                for j in range(KC):
                    nc.tensor.matmul(out, ctxw[:, j, b].rearrange("p h s -> p (h s)"), W[:, 2, j, :],
                                     start=(j == 0), stop=False)
                nc.tensor.matmul(out, k.cst[0:1, C_ONE:C_ONE + HW], bv[:], start=False, stop=True).then_inc(v_ready, 1)

            for i in range(B + 1):
                if i < B:
                    if i > 0:
                        pe.wait_ge(q_done, KC * i)
                        norm.pe_transpose(pe, i, BT)
                    pe.wait_ge(norm.xl_done, i + 1)
                    pe.wait_ge(wl_done, 1)
                    for c in range(KC):
                        for j in range(KC):
                            last = matmul3(nc, ps[:, BT + c, :], wqh[:, j, c * P:(c + 1) * P],
                                           wql[:, j, c * P:(c + 1) * P], norm.xh[:, i % 2, j], norm.xl[:, i % 2, j],
                                           j == 0, j == KC - 1)
                    last.then_inc(q_ready, 1)
                    pe.wait_ge(q_done, KC * (i + 1))
                    if i == 0:
                        pe.wait_ge(kbd_done, KC)
                    else:
                        pe.wait_ge(s_read, i)
                    for t in range(TB):
                        for c in range(KC):
                            at = t * HW + c * HW // 2
                            last = nc.tensor.matmul(ps[:, BS, at:at + HW // 2], qT[:, i % 2, c, t * P:(t + 1) * P],
                                                    kbd[:, c, i].rearrange("p h s -> p (h s)"), start=True, stop=True)
                    last.then_inc(s_ready, 1)
                if i >= 1:
                    b = i - 1
                    pe.wait_ge(p_done, b + 1)
                    if b == 0:
                        pe.wait_ge(v_done, B)
                    else:
                        pe.wait_ge(pt_done, b)
                    for t in range(TB):
                        last = nc.tensor.transpose(ps[0:HW, BP, t * P:(t + 1) * P],
                                                   E[:, b % 2, t * H:(t + 1) * H, :].rearrange("p h s -> p (h s)"),
                                                   k.ident)
                    last.then_inc(pt_ready, 1)
                    pe.wait_ge(pt_done, b + 1)
                    if b > 0:
                        pe.wait_ge(otl_done, b)
                    for c in range(KC):
                        last = nc.tensor.matmul(ps[:, BO + c, :],
                                                vbd[:, b].rearrange("p h d -> p (h d)")[:, c * P:(c + 1) * P],
                                                pT[:, b % 2], start=True, stop=True)
                    last.then_inc(ot_ready, 1)
                    pe.wait_ge(otl_done, b + 1)
                    pe.wait_ge(wl_done, 2)
                    if b > 0:
                        pe.wait_ge(y_done, b)
                    else:
                        pe.wait_ge(k_copied, KC)
                    for t in range(TB):
                        for j in range(KC):
                            last = matmul3(nc, ps[:, BY + t // 2, (t % 2) * D:(t % 2 + 1) * D],
                                           oth[:, b % 2, j, t * P:(t + 1) * P], otl[:, b % 2, j, t * P:(t + 1) * P],
                                           woh[:, j], wol[:, j], j == 0, j == KC - 1)
                    last.then_inc(y_ready, 1)


def experts_ffn(k, layer):
    if layer == 0:
        dense_ffn(k, layer=0)
    with ExitStack() as ctx:
        hid = 256 if layer == 0 else 704
        m = Experts(k, ctx, layer, 9 if layer == 1 else 8, hid)
        route(k, m)
        run_experts(k, m)
        combine(k, m)


class Experts:

    def __init__(self, k, ctx, layer, n, hid):
        nc = k.nc
        self.layer, self.n, self.hid = layer, n, hid
        self.tag = f"f{layer}"
        self.tiles = (B * S * 2 - n) // P + n
        self.halves = 2 if hid > 512 else 1
        self.hcols = hid // self.halves
        self.chunks = -(-hid // P)
        self.wcols = KC * 2 * hid + self.chunks * D
        sb = lambda n, s, d=F32: ctx.enter_context(nc.sbuf_tensor(f"{self.tag}_{n}", s, d))
        sem = lambda n: k.sem(f"{self.tag}_{n}")
        self.sb, self.sem = sb, sem
        self.slot = sb("slot", [P, 2, NT], I32)
        self.wt = sb("wt", [P, 2, NT])
        self.expert_of = sb("expert_of", [P, 44], I32)
        self.buffer_of = sb("buffer_of", [P, 44], I32)
        self.done_at = sb("done_at", [P, n], I32)
        self.raw = sb("raw", [P, 2, self.wcols])
        self.wh = sb("wh", [P, 2, self.wcols], F32R)
        self.wl = sb("wl", [P, 2, self.wcols], F32R)
        self.raw_landed = [sem("raw_landed0"), sem("raw_landed1")]
        self.w_hi, self.w_ready = sem("weights_hi"), sem("weights_ready")

    def pool_load(self, k, e):
        k.nc.gpsimd.dma_start(self.raw[:, e % 2], k.ins[f"we_{self.tag}"][e]).then_inc(self.raw_landed[e % 2], 16)

    def pool_split(self, k, pool, e):
        nc, raw, b = k.nc, self.raw, e % 2
        pool.wait_ge(self.raw_landed[b], 16 * (e // 2 + 1))
        nc.gpsimd.tensor_scalar(self.wh[:, b], raw[:, b], 1.0, 0.0, ALU.mult, ALU.add).then_inc(self.w_hi, 1)
        pool.wait_ge(self.w_hi, e + 1)
        nc.gpsimd.tensor_tensor(self.wl[:, b], raw[:, b], self.wh[:, b].bitcast(F32),
                                ALU.subtract).then_inc(self.w_ready, 1)


def route(k, m):
    nc, ps, n, layer = k.nc, k.ps, m.n, m.layer
    reuse = layer == 0
    with ExitStack() as ctx:
        sb = lambda n, s, d=F32: ctx.enter_context(nc.sbuf_tensor(f"r{layer}_{n}", s, d))
        sem = lambda n: k.sem(f"r{layer}_{n}")
        norm = Norm(k, sb, sem, "n", False, reuse)
        gate_w = sb("gate_w", [P, KC, n])
        extra = sb("extra", [P, D + 1])
        L, M = sb("L", [P, NT, n]), sb("M", [P, NT + 1, n])
        Q, R = sb("Q", [P, NT, n]), sb("R", [P, NT, n])
        M1, M2 = sb("M1", [P, NT, n]), sb("M2", [P, NT, n])
        pos = sb("pos", [P, NT + 1, n])
        v = sb("v", [P, 8, NT])
        cnt = sb("cnt", [P, n], I32)
        tiles, ends, base = sb("tiles", [P, n]), sb("ends", [P, n]), sb("base", [P, n])
        cmp = sb("cmp", [P, 40, n])
        tile_e = sb("tile_e", [P, 40])
        ss = sb("ss", [P, NT])
        rr = sb("rr", [P, 5, TB])
        junk = sb("junk", [P, D])
        loaded, dstep, xt_used = sem("loaded"), sem("dve_step"), sem("logits_ready")
        exp_in, exp_out, m_done, pos_ready = sem("exp_in"), sem("exp_out"), sem("m_done"), sem("pos_ready")
        sq_done, rescaled, alpha = sem("sq_done"), sem("rescaled"), sem("alpha")
        n_loads = {0: 1, 1: 2, 2: 3}[layer]
        BT, BL, BC = 0, 2, 3
        block = ctx.enter_context(nc.Block())

        @block.sync
        def _(sp):
            sp.dma_start(gate_w[:], k.ins[f"gate_f{layer}"]).then_inc(loaded, 16)
            if layer == 1:
                sp.dma_start(extra[:, 0:n], k.ins["gbias_f1"].unsqueeze(0).to_broadcast([P, n])).then_inc(loaded, 16)
            if layer == 2:
                sp.dma_start(extra[:, 0:D], k.ins["nw_f2"].unsqueeze(0).to_broadcast([P, D])).then_inc(loaded, 16)
                sp.dma_start(extra[:, D:D + 1], k.ins["alpha_f2"].unsqueeze(0).to_broadcast([P, 1])).then_inc(loaded, 16)
            sp.wait_ge(loaded, 16 * n_loads)

        @block.gpsimd
        def _(pool):
            m.pool_load(k, 0)
            m.pool_load(k, 1)
            m.pool_split(k, pool, 0)
            m.pool_split(k, pool, 1)

        @block.scalar
        def _(act):
            for b in range(B):
                if layer == 2:
                    act.wait_ge(norm.normed, TB * (b + 1))
                    for t in range(b * TB, (b + 1) * TB):
                        if t:
                            act.wait_ge(sq_done, t)
                        nc.scalar.activation(junk[:], k.XN[:, t, :], ACT.Square,
                                             accum_out=ss[:, t:t + 1]).then_inc(sq_done, 1)
                if b >= 2:
                    act.wait_ge(xt_used, b - 1)
                norm.act_evacuate(act, b, BT)
            act.wait_ge(exp_in, 1)
            nc.scalar.activation(L[:], L[:], ACT.Exp, scale=-1.0 if layer == 1 else 1.0).then_inc(exp_out, 1)

        @block.tensor
        def _(pe):
            for b in range(B):
                if b:
                    pe.wait_ge(norm.xh_done, b)
                if layer == 2:
                    pe.wait_ge(rescaled, TB * (b + 1))
                norm.pe_transpose(pe, b, BT)
                pe.wait_ge(norm.xh_done, b + 1)
                if b == 0:
                    pe.wait_ge(loaded, 16 * n_loads)
                for i in range(TB):
                    t = b * TB + i
                    for j in range(KC):
                        last = nc.tensor.matmul(ps[:, BL, t * n:(t + 1) * n], norm.xf[:, b % 2, j, i * P:(i + 1) * P],
                                                gate_w[:, j], start=(j == 0), stop=(j == KC - 1))
                last.then_inc(xt_used, 1)
            pe.wait_ge(m_done, 1)
            nc.tensor.matmul(ps[:, BC, 0:(NT + 1) * n], k.cst[:, C_TRI:C_TRI + P], M[:].rearrange("p t e -> p (t e)"),
                             start=True, stop=False)
            for t in range(NT):
                out = ps[:, BC, (t + 1) * n:(NT + 1) * n].rearrange("p (t e) -> p t e", e=n)
                last = nc.tensor.matmul(out, k.cst[:, C_ONE:C_ONE + P],
                                        M[:, t:t + 1, :].to_broadcast([P, NT - t, n]), start=False, stop=(t == NT - 1))
            last.then_inc(pos_ready, 1)

        @block.vector
        def _(dve):
            ch = Chain(dve, dstep)
            if layer == 2:
                dve.wait_ge(loaded, 16 * n_loads)
                al = extra[:, D:D + 1]
                ch.link(nc.vector.tensor_scalar(al, al, -0.5, 2.0, ALU.max, ALU.min))
                ch.link(nc.vector.tensor_scalar(al, al, k.tg[:, 6:7], None, ALU.mult))
            if not reuse:
                for b in range(B):
                    norm.dve_norm(dve, b)
                    if layer == 2:
                        t0 = b * TB
                        xb, nb = k.X[:, t0:t0 + TB, :], k.XN[:, t0:t0 + TB, :]
                        dve.wait_ge(norm.normed, TB * (b + 1))
                        ch.add(nc.vector.scalar_tensor_tensor(xb, nb, k.tg[:, 6:7], xb, ALU.mult, ALU.add))
                        dve.wait_ge(sq_done, t0 + TB)
                        ch.link(nc.vector.tensor_scalar(rr[:, 0], ss[:, t0:t0 + TB], 1.0 / D, 1e-6, ALU.mult, ALU.add))
                        norm.rsqrt(dve, rr[:, 0], rr[:, 1], rr[:, 2], rr[:, 3], rr[:, 4].bitcast(I32))
                        for i in range(TB):
                            nc.vector.scalar_tensor_tensor(k.XN[:, t0 + i, :], k.XN[:, t0 + i, :], rr[:, 1, i:i + 1],
                                                           extra[:, 0:D], ALU.mult, ALU.mult).then_inc(rescaled, 1)
            ch.link(nc.vector.memset(M[:, NT:NT + 1, :], 0.0))
            dve.wait_ge(xt_used, B)
            lg = ps[:, BL, 0:NT * n].rearrange("p (t e) -> p t e", e=n)
            row = lambda a: a.unsqueeze(2).to_broadcast([P, NT, n])
            col = lambda a: a.unsqueeze(1).to_broadcast([P, NT, n])
            if layer == 1:
                dve.wait_ge(loaded, 16 * n_loads)
                nc.vector.tensor_tensor(L[:], lg, col(extra[:, 0:n]), ALU.add).then_inc(exp_in, 1)
                dve.wait_ge(exp_out, 1)
                ch.link(nc.vector.tensor_scalar(Q[:], L[:], 1.0, None, ALU.add))
                ch.link(nc.vector.reciprocal(Q[:], Q[:]))
            else:
                ch.link(nc.vector.tensor_reduce(v[:, 0], lg, AX.X, ALU.max))
                nc.vector.tensor_tensor(L[:], lg, row(v[:, 0]), ALU.subtract).then_inc(exp_in, 1)
                dve.wait_ge(exp_out, 1)
                ch.link(nc.vector.tensor_reduce(v[:, 0], L[:], AX.X, ALU.add))
                ch.link(nc.vector.reciprocal(v[:, 0], v[:, 0]))
                ch.link(nc.vector.tensor_tensor(Q[:], L[:], row(v[:, 0]), ALU.mult))
            rev = col(k.cst[:, C_REV:C_REV + n])

            def choose(score, top, mask):
                ch.link(nc.vector.tensor_reduce(top, score, AX.X, ALU.max))
                ch.link(nc.vector.tensor_tensor(R[:], score, row(top), ALU.is_equal))
                ch.link(nc.vector.tensor_tensor(R[:], R[:], rev, ALU.mult))
                ch.link(nc.vector.tensor_reduce(v[:, 7], R[:], AX.X, ALU.max))
                ch.link(nc.vector.tensor_tensor(mask, R[:], row(v[:, 7]), ALU.is_equal))

            choose(Q[:], v[:, 1], M1[:])
            ch.link(nc.vector.scalar_tensor_tensor(Q[:], M1[:], -4.0, Q[:], ALU.mult, ALU.add))
            choose(Q[:], v[:, 2], M2[:])
            nc.vector.tensor_tensor(M[:, 0:NT, :], M1[:], M2[:], ALU.add).then_inc(m_done, 1)
            ch.link(nc.vector.tensor_tensor(v[:, 3], v[:, 1], v[:, 2], ALU.add))
            if layer < 2:
                ch.link(nc.vector.tensor_scalar(v[:, 3], v[:, 3], 1e-20, None, ALU.add))
            ch.link(nc.vector.reciprocal(v[:, 3], v[:, 3]))
            ch.link(nc.vector.tensor_scalar(v[:, 3], v[:, 3], extra[:, D:D + 1] if layer == 2 else
                                            k.tg[:, 4 + layer:5 + layer], None, ALU.mult))
            dve.wait_ge(pos_ready, 1)
            ch.link(nc.vector.tensor_copy(pos[:], ps[:, BC, 0:(NT + 1) * n].rearrange("p (t e) -> p t e", e=n)))
            ch.link(nc.vector.tensor_scalar(cnt[:], pos[:, NT], float(P - 1), None, ALU.add))
            ch.link(nc.vector.tensor_scalar(cnt[:], cnt[:], 7, None, ALU.logical_shift_right))
            ch.link(nc.vector.tensor_copy(tiles[:], cnt[:]))
            ch.link(nc.vector.tensor_tensor_scan(ends[:], k.cst[:, C_ONE:C_ONE + n], tiles[:], 0.0, ALU.mult, ALU.add))
            ch.link(nc.vector.tensor_tensor(base[:], ends[:], tiles[:], ALU.subtract))
            ch.link(nc.vector.tensor_scalar(base[:], base[:], float(P), None, ALU.mult))
            ch.link(nc.vector.tensor_tensor(R[:], pos[:, 0:NT, :], col(base[:]), ALU.add))
            for s, mask in enumerate((M1, M2)):
                ch.link(nc.vector.tensor_tensor(Q[:], mask[:], R[:], ALU.mult))
                ch.link(nc.vector.tensor_reduce(v[:, 4], Q[:], AX.X, ALU.add))
                ch.link(nc.vector.tensor_copy(m.slot[:, s], v[:, 4]))
                if layer == 0:
                    capacity = -(-5 * B * S * 2 // (4 * n))
                    ch.link(nc.vector.tensor_tensor(Q[:], mask[:], pos[:, 0:NT, :], ALU.mult))
                    ch.link(nc.vector.tensor_reduce(v[:, 4], Q[:], AX.X, ALU.add))
                    ch.link(nc.vector.tensor_scalar(v[:, 4], v[:, 4], float(capacity), None, ALU.is_lt))
                    ch.link(nc.vector.tensor_tensor(v[:, 1 + s], v[:, 1 + s], v[:, 4], ALU.mult))
                ch.link(nc.vector.tensor_tensor(m.wt[:, s], v[:, 1 + s], v[:, 3], ALU.mult))
            shape = [P, 40, n]
            ch.link(nc.vector.tensor_tensor(cmp[:], ends[:].unsqueeze(1).to_broadcast(shape),
                                            k.cst[:, C_J:C_J + 40].unsqueeze(2).to_broadcast(shape), ALU.is_le))
            ch.link(nc.vector.tensor_reduce(tile_e[:], cmp[:], AX.X, ALU.add))
            ch.link(nc.vector.tensor_scalar(m.expert_of[:, 0:40], tile_e[:], float(n - 1), None, ALU.min))
            ch.link(nc.vector.tensor_scalar(m.buffer_of[:, 0:40], m.expert_of[:, 0:40], 1, None, ALU.bitwise_and))
            ch.link(nc.vector.tensor_scalar(m.done_at[:], ends[:], 1.0, None, ALU.add))


def run_experts(k, m):
    nc, ps, n = k.nc, k.ps, m.n
    NJ, NH, HC, NC_ = m.tiles, m.halves, m.hcols, m.chunks
    last_k = m.hid - (NC_ - 1) * P
    with ExitStack() as ctx:
        sb = lambda n, s, d=F32: ctx.enter_context(nc.sbuf_tensor(f"e{m.layer}_{n}", s, d))
        sem = lambda n: k.sem(f"e{m.layer}_{n}")
        xs = sb("xs", [P, 2, D])
        xh, xl = sb("xh", [P, 2, KC, P], F32R), sb("xl", [P, 2, KC, P], F32R)
        sg = sb("sg", [P, 2, HC])
        h = sb("h", [P, 2, m.hid])
        hth, htl = sb("hth", [P, 2, NC_, P], F32R), sb("htl", [P, 2, NC_, P], F32R)
        y = sb("y", [P, 2, D])
        scattered, buffer_free = sem("scattered"), sem("buffer_free")
        landed, stored = [sem("landed0"), sem("landed1")], [sem("stored0"), sem("stored1")]
        xt_ready, xh_done, xl_done = sem("xt_ready"), sem("xh_done"), sem("xl_done")
        g_ready, sg_done, h_done = sem("g_ready"), sem("sg_done"), sem("h_done")
        ht_ready, hth_done, htl_done = sem("ht_ready"), sem("hth_done"), sem("htl_done")
        y_ready, y_done = sem("y_ready"), sem("y_done")
        BG, BH, BX, BY = 0, 4, 6, 7
        gu = lambda w: w[:, :, 0:KC * 2 * m.hid].rearrange("p b (c f) -> p b c f", c=KC)
        dn = lambda w: w[:, :, KC * 2 * m.hid:].rearrange("p b (c f) -> p b c f", f=D)
        rounds = (NJ - 1) // 2
        rest = NJ - 1 - 2 * rounds
        xrows = k.xs_dram.rearrange("(j p) d -> p j d", p=P)
        yrows = k.y_dram.rearrange("(j p) d -> p j d", p=P)
        block = ctx.enter_context(nc.Block())

        @block.gpsimd
        def _(pool):
            for t in range(NT):
                for s in range(2):
                    nc.gpsimd.indirect_dma_start(
                        out=k.xs_dram, out_offset=bass.IndirectOffsetOnAxis(ap=m.slot[:, s, t:t + 1], axis=0),
                        in_=k.XN[:, t, :], in_offset=None).then_inc(scattered, 16)
            m.pool_load(k, 2)
            m.pool_load(k, 3)
            for e in range(2, n):
                end = pool.value_load(m.done_at[0:1, e - 2:e - 1], min_val=1, max_val=NJ + 1)
                pool.wait_ge(y_ready, end)
                pool.sem_inc(buffer_free, 1)
                m.pool_split(k, pool, e)
                if e + 2 < n:
                    pool.wait_ge(m.w_ready, e + 1)
                    m.pool_load(k, e + 2)

        @block.sync
        def _(sp):
            for p in range(2):
                sp.sem_inc(stored[p], 16)
            sp.wait_ge(scattered, 32 * 16)
            for j in range(2):
                sp.dma_start(xs[:, j], xrows[:, j]).then_inc(landed[j], 16)

            def step(j, p, load=True):
                if load:
                    sp.wait_ge(xt_ready, j + 1)
                    sp.dma_start(xs[:, p], xrows[:, bass.ds(j + 2, 1), :] .rearrange("p o d -> p (o d)")).then_inc(landed[p], 16)
                sp.wait_ge(y_done, j + 1)
                sp.dma_start(yrows[:, bass.ds(j, 1), :].rearrange("p o d -> p (o d)"), y[:, p]).then_inc(stored[p], 16)

            pairs = (NJ - 2) // 2
            with sp.Fori(0, 2 * pairs, 2) as j:
                for u in range(2):
                    step(j + u, u)
            for j in range(2 * pairs, NJ):
                step(j, j % 2, load=(j + 2 < NJ + 1 - rest))
            for p in range(2):
                sp.wait_ge(stored[p], 16 * ((NJ + 1 - p) // 2) + 16)

        @block.scalar
        def _(act):
            def x_high(j, p):
                act.wait_ge(xt_ready, j + 1)
                nc.scalar.activation(xh[:, p], ps[:, BX, 0:D].rearrange("p (c q) -> p c q", c=KC),
                                     ACT.Copy).then_inc(xh_done, 1)

            def silu(j, p):
                for i in range(NH):
                    g = NH * j + i
                    q = i if NH == 2 else p
                    act.wait_ge(g_ready, g + 1)
                    nc.scalar.activation(sg[:, q], ps[:, BG + 2 * q, 0:HC], ACT.Silu).then_inc(sg_done, 1)

            def output(j, p):
                act.wait_ge(y_ready, j + 2)
                act.wait_ge(stored[p], j // 2 * 16 + 16 if isinstance(j, int) else (j - p) * 8 + 16)
                nc.scalar.activation(y[:, p], ps[:, BY, 0:D], ACT.Copy).then_inc(y_done, 1)

            def h_high(j, p):
                act.wait_ge(ht_ready, j + 1)
                full = NC_ if last_k == P else NC_ - 1
                src = ps[:, BH:BH + 2, :].rearrange("p a (c q) -> p (a c) q", q=P)
                ins = nc.scalar.activation(hth[:, p, 0:full], src[:, 0:full], ACT.Copy)
                if full < NC_:
                    ins = nc.scalar.activation(hth[0:last_k, p, full], src[0:last_k, full], ACT.Copy)
                ins.then_inc(hth_done, 1)

            def step(j, p, more=True):
                silu(j, p)
                if not isinstance(j, int) or j >= 1:
                    output(j - 1, 1 - p)
                if more:
                    x_high(j + 1, 1 - p)
                h_high(j, p)

            x_high(0, 0)
            for j in range(1):
                step(0, 0)
            with act.Fori(1, 1 + 2 * rounds, 2) as j:
                for u in range(2):
                    step(j + u, 1 - u)
            if rest:
                step(NJ - 1, (NJ - 1) % 2, more=False)
            output(NJ - 1, (NJ - 1) % 2)

        @block.vector
        def _(dve):
            def x_low(j, p):
                dve.wait_ge(xh_done, j + 1)
                nc.vector.tensor_tensor(xl[:, p], ps[:, BX, 0:D].rearrange("p (c q) -> p c q", c=KC),
                                        xh[:, p].bitcast(F32), ALU.subtract).then_inc(xl_done, 1)

            def step(j, p, more=True):
                for i in range(NH):
                    q = i if NH == 2 else p
                    dve.wait_ge(sg_done, NH * j + i + 1)
                    nc.vector.tensor_tensor(h[:, p, i * HC:(i + 1) * HC], ps[:, BG + 2 * q + 1, 0:HC], sg[:, q],
                                            ALU.mult).then_inc(h_done, 1)
                if more:
                    x_low(j + 1, 1 - p)
                dve.wait_ge(hth_done, j + 1)
                full = NC_ if last_k == P else NC_ - 1
                src = ps[:, BH:BH + 2, :].rearrange("p a (c q) -> p (a c) q", q=P)
                ins = nc.vector.tensor_tensor(htl[:, p, 0:full], src[:, 0:full], hth[:, p, 0:full].bitcast(F32),
                                              ALU.subtract)
                if full < NC_:
                    ins = nc.vector.tensor_tensor(htl[0:last_k, p, full], src[0:last_k, full],
                                                  hth[0:last_k, p, full].bitcast(F32), ALU.subtract)
                ins.then_inc(htl_done, 1)

            x_low(0, 0)
            step(0, 0)
            with dve.Fori(1, 1 + 2 * rounds, 2) as j:
                for u in range(2):
                    step(j + u, 1 - u)
            if rest:
                step(NJ - 1, (NJ - 1) % 2, more=False)

        @block.tensor
        def _(pe):
            pe.sem_inc(y_ready, 1)

            def buffer(j):
                at = bass.ds(j, 1)
                return pe.value_load(m.buffer_of[0:1, at], min_val=0, max_val=1)

            def x_transpose(j, p):
                pe.wait_ge(landed[p], 16 * (j // 2 + 1) if isinstance(j, int) else (j - p) * 8 + 16)
                if not isinstance(j, int) or j >= 1:
                    pe.wait_ge(xl_done, j)
                for c in range(KC):
                    last = nc.tensor.transpose(ps[:, BX, c * P:(c + 1) * P], xs[:, p, c * P:(c + 1) * P], k.ident)
                last.then_inc(xt_ready, 1)

            def gate_up(j, p):
                e = pe.value_load(m.expert_of[0:1, bass.ds(j, 1)], min_val=0, max_val=n - 1)
                b = bass.ds(buffer(j), 1)
                pe.wait_ge(m.w_ready, e + 1)
                pe.wait_ge(xl_done, j + 1)
                for i in range(NH):
                    g = NH * j + i
                    q = i if NH == 2 else p
                    if not isinstance(j, int) or g >= 2:
                        pe.wait_ge(h_done, g - 1)
                    for s in range(2):
                        at = s * m.hid + i * HC
                        for c in range(KC):
                            last = matmul3(nc, ps[:, BG + 2 * q + s, 0:HC], xh[:, p, c], xl[:, p, c],
                                           gu(m.wh)[:, b, c, at:at + HC].rearrange("p o f -> p (o f)"),
                                           gu(m.wl)[:, b, c, at:at + HC].rearrange("p o f -> p (o f)"),
                                           c == 0, c == KC - 1)
                    last.then_inc(g_ready, 1)

            def down(j, p):
                b = bass.ds(buffer(j), 1)
                pe.wait_ge(htl_done, j + 1)
                if not isinstance(j, int) or j >= 1:
                    pe.wait_ge(y_done, j)
                for c in range(NC_):
                    r = P if c < NC_ - 1 else last_k
                    last = matmul3(nc, ps[:, BY, 0:D], hth[0:r, p, c], htl[0:r, p, c],
                                   dn(m.wh)[0:r, b, c].rearrange("p o f -> p (o f)"),
                                   dn(m.wl)[0:r, b, c].rearrange("p o f -> p (o f)"), c == 0, c == NC_ - 1)
                last.then_inc(y_ready, 1)

            def h_transpose(j, p):
                pe.wait_ge(h_done, NH * j + NH)
                if not isinstance(j, int) or j >= 1:
                    pe.wait_ge(htl_done, j)
                for c in range(NC_):
                    r = P if c < NC_ - 1 else last_k
                    last = nc.tensor.transpose(ps[0:r, BH + c // 4, (c % 4) * P:(c % 4 + 1) * P],
                                               h[:, p, c * P:c * P + r], k.ident)
                last.then_inc(ht_ready, 1)

            def step(j, p, more=True):
                gate_up(j, p)
                if not isinstance(j, int) or j >= 1:
                    down(j - 1, 1 - p)
                if more:
                    x_transpose(j + 1, 1 - p)
                h_transpose(j, p)

            x_transpose(0, 0)
            step(0, 0)
            with pe.Fori(1, 1 + 2 * rounds, 2) as j:
                for u in range(2):
                    step(j + u, 1 - u)
            if rest:
                step(NJ - 1, (NJ - 1) % 2, more=False)
            down(NJ - 1, (NJ - 1) % 2)


def combine(k, m):
    nc = k.nc
    with ExitStack() as ctx:
        depth = 4
        rows = ctx.enter_context(nc.sbuf_tensor(f"c{m.layer}_rows", [P, depth, 2, D], F32))
        gathered = [k.sem(f"c{m.layer}_gathered{i}") for i in range(depth)]
        first = k.sem(f"c{m.layer}_first")
        added = k.sem(f"c{m.layer}_added")
        block = ctx.enter_context(nc.Block())

        @block.gpsimd
        def _(pool):
            for t in range(NT):
                if t >= depth:
                    pool.wait_ge(added, t - depth + 1)
                for s in range(2):
                    nc.gpsimd.indirect_dma_start(
                        out=rows[:, t % depth, s], out_offset=None, in_=k.y_dram[0:m.tiles * P],
                        in_offset=bass.IndirectOffsetOnAxis(ap=m.slot[:, s, t:t + 1], axis=0)
                    ).then_inc(gathered[t % depth], 16)

        @block.vector
        def _(dve):
            for t in range(NT):
                dve.wait_ge(gathered[t % depth], 32 * (t // depth + 1))
                x = k.X[:, t, :]
                nc.vector.scalar_tensor_tensor(x, rows[:, t % depth, 0], m.wt[:, 0, t:t + 1], x,
                                               ALU.mult, ALU.add).then_inc(first, 1)
                dve.wait_ge(first, t + 1)
                nc.vector.scalar_tensor_tensor(x, rows[:, t % depth, 1], m.wt[:, 1, t:t + 1], x,
                                               ALU.mult, ALU.add).then_inc(added, 1)


def dense_ffn(k, layer=3):
    nc, ps = k.nc, k.ps
    quantised = layer == 3
    hid = 768 if quantised else 512
    nch = hid // P
    gate = k.tg[:, 4 + layer:5 + layer]
    with ExitStack() as ctx:
        sb = lambda n, s, d=F32: ctx.enter_context(nc.sbuf_tensor(f"d{layer}_{n}", s, d))
        sem = lambda n: k.sem(f"d{layer}_{n}")
        norm = Norm(k, sb, sem, "n", True)
        wgu, wdn = sb("wgu", [P, KC, 2 * hid]), sb("wdn", [P, nch, D])
        gh, gl = sb("gh", [P, KC, 2 * hid], F32R), sb("gl", [P, KC, 2 * hid], F32R)
        dh, dl = sb("dh", [P, nch, D], F32R), sb("dl", [P, nch, D], F32R)
        sg, h = sb("sg", [P, 2, S]), sb("h", [P, 2, S])
        hh, hl = sb("hh", [P, 2, nch, S], F32R), sb("hl", [P, 2, nch, S], F32R)
        loaded = [sem("loaded_gate_up"), sem("loaded_down")]
        scaled, whi, wlo = sem("weights_scaled"), sem("weights_hi"), sem("weights_lo")
        g_ready, sg_done, h_done = sem("g_ready"), sem("sg_done"), sem("h_done")
        hh_done, hl_done, y_ready, y_done = sem("hh_done"), sem("hl_done"), sem("y_ready"), sem("y_done")
        BT, BG, BY = 0, 2, 6
        block = ctx.enter_context(nc.Block())

        @block.sync
        def _(sp):
            dst = (wgu[:].bitcast(I32), wdn[:].bitcast(I32)) if quantised else (wgu[:], wdn[:])
            sp.dma_start(dst[0], k.ins[f"wd_f{layer}"]).then_inc(loaded[0], 16)
            sp.dma_start(dst[1], k.ins[f"wo_f{layer}"]).then_inc(loaded[1], 16)
            for s in loaded:
                sp.wait_ge(s, 16)

        @block.gpsimd
        def _(pool):
            for i, (w, hi, lo) in enumerate(((wgu, gh, gl), (wdn, dh, dl))):
                pool.wait_ge(whi, i + 1)
                nc.gpsimd.tensor_tensor(lo[:], w[:], hi[:].bitcast(F32), ALU.subtract).then_inc(wlo, 1)
            for b in range(B):
                for c in range(nch):
                    g = b * nch + c
                    pool.wait_ge(hh_done, g + 1)
                    nc.gpsimd.tensor_tensor(hl[:, b % 2, c], h[:, g % 2], hh[:, b % 2, c].bitcast(F32),
                                            ALU.subtract).then_inc(hl_done, 1)

        @block.scalar
        def _(act):
            for i, (w, hi) in enumerate(((wgu, gh), (wdn, dh))):
                act.wait_ge(loaded[i], 16)
                if quantised:
                    act.wait_ge(scaled, i + 1)
                nc.scalar.activation(hi[:], w[:], ACT.Copy).then_inc(whi, 1)
                if i == 0:
                    norm.act_evacuate(act, 0, BT)
            for g in range(B * nch + 1):
                if g < B * nch:
                    act.wait_ge(g_ready, g + 1)
                    if g >= 2:
                        act.wait_ge(h_done, g - 1)
                    nc.scalar.activation(sg[:, g % 2], ps[:, BG + 2 * (g % 2), :], ACT.Silu).then_inc(sg_done, 1)
                    if g % nch == 1 and g // nch + 1 < B:
                        norm.act_evacuate(act, g // nch + 1, BT)
                if g >= 1:
                    u = g - 1
                    act.wait_ge(h_done, u + 1)
                    nc.scalar.activation(hh[:, (u // nch) % 2, u % nch], h[:, u % 2], ACT.Copy).then_inc(hh_done, 1)

        @block.vector
        def _(dve):
            norm.dve_norm(dve, 0)
            if quantised:
                for i, w in enumerate((wgu, wdn)):
                    dve.wait_ge(loaded[i], 16)
                    nc.vector.tensor_scalar(w[:], w[:].bitcast(I32), 1.0 / 127.0, None, ALU.mult).then_inc(scaled, 1)
            norm.dve_low(dve, 0, BT)

            def outputs(b):
                for t in range(b * TB, (b + 1) * TB):
                    dve.wait_ge(y_ready, t + 1)
                    nc.vector.scalar_tensor_tensor(k.X[:, t, :], ps[:, BY + t % 2, 0:D], gate, k.X[:, t, :],
                                                   ALU.mult, ALU.add).then_inc(y_done, 1)

            for b in range(B):
                for c in range(nch):
                    g = b * nch + c
                    dve.wait_ge(sg_done, g + 1)
                    if g >= 2:
                        dve.wait_ge(hl_done, g - 1)
                    nc.vector.tensor_tensor(h[:, g % 2], ps[:, BG + 2 * (g % 2) + 1, :], sg[:, g % 2],
                                            ALU.mult).then_inc(h_done, 1)
                    if c == 0 and b + 1 < B:
                        norm.dve_norm(dve, b + 1)
                    if c == 1 and b + 1 < B:
                        norm.dve_low(dve, b + 1, BT)
                    if c == 1 and b >= 1:
                        outputs(b - 1)
            outputs(B - 1)

        @block.tensor
        def _(pe):
            def outputs(b):
                pe.wait_ge(hl_done, nch * (b + 1))
                pe.wait_ge(wlo, 2)
                for t in range(b * TB, (b + 1) * TB):
                    if t >= 2:
                        pe.wait_ge(y_done, t - 1)
                    q = slice((t % TB) * P, (t % TB + 1) * P)
                    for c in range(nch):
                        last = matmul3(nc, ps[:, BY + t % 2, 0:D], hh[:, b % 2, c, q], hl[:, b % 2, c, q],
                                       dh[:, c], dl[:, c], c == 0, c == nch - 1)
                    last.then_inc(y_ready, 1)

            norm.pe_transpose(pe, 0, BT)
            pe.wait_ge(wlo, 1)
            for b in range(B):
                pe.wait_ge(norm.xl_done, b + 1)
                for c in range(nch):
                    g = b * nch + c
                    if g >= 2:
                        pe.wait_ge(h_done, g - 1)
                    for s in range(2):
                        for j in range(KC):
                            at = slice(s * hid + c * P, s * hid + (c + 1) * P)
                            last = matmul3(nc, ps[:, BG + 2 * (g % 2) + s, :], gh[:, j, at], gl[:, j, at],
                                           norm.xh[:, b % 2, j], norm.xl[:, b % 2, j], j == 0, j == KC - 1)
                    last.then_inc(g_ready, 1)
                    if c == 0 and b + 1 < B:
                        norm.pe_transpose(pe, b + 1, BT)
                    if c == 1 and b >= 1:
                        outputs(b - 1)
            outputs(B - 1)


def two_way_attention(k):
    nc, ps = k.nc, k.ps
    gate = k.tg[:, 2:3]
    QC, KS, VS, QS, KCH, VC = range(6)
    with ExitStack() as ctx:
        sb = lambda n, s, d=F32: ctx.enter_context(nc.sbuf_tensor(f"a2_{n}", s, d))
        sem = lambda n: k.sem(f"a2_{n}")
        norm = Norm(k, sb, sem, "n", True)
        W = sb("w", [P, 6, KC, D])
        WG = sb("wg", [P, 4, D])
        Wh, Wl = sb("wh", [P, 3, KC, D], F32R), sb("wl", [P, 3, KC, D], F32R)
        bt = sb("bt", [P, 4, KC])
        br = sb("br", [1, 3 * D])
        ksT, qsT = sb("ksT", [P, KC, B * SK]), sb("qsT", [P, KC, B * SK])
        vs = sb("vs", [SK, B, D])
        qT, kcT = sb("qT", [P, KC, S]), sb("kcT", [P, KC, S])
        vc = sb("vc", [P, TB, D])
        e1 = sb("e1", [P, TB, SK])
        m1, r1 = sb("m1", [P, TB]), sb("r1", [P, TB])
        e2 = sb("e2", [SK, S])
        m2, r2 = sb("m2", [SK, 1]), sb("r2", [SK, 1])
        p1T = sb("p1T", [SK, S])
        p2T = sb("p2T", [P, TB, SK])
        s2c = sb("s2c", [SK, D])
        cT, sT = sb("cT", [P, KC, S]), sb("sT", [P, KC, S])
        g = sb("g", [P, 2, D])
        s2 = sb("s2", [P, 2, D])
        df = sb("df", [P, 2, D])

        loaded, dstep = sem("loaded"), sem("dve_step")
        whi, wl_done, ctx_ready, ctx_done = sem("weights_hi"), sem("weights_lo"), sem("ctx_ready"), sem("ctx_done")
        vs_ready, vs_done = sem("vs_ready"), sem("vs_done")
        q_ready, q_done, k_ready, k_done = sem("q_ready"), sem("q_done"), sem("k_ready"), sem("k_done")
        v_ready, v_done = sem("v_ready"), sem("v_done")
        s1_ready, sub_done, exp1_done, p1_done = sem("s1_ready"), sem("sub_done"), sem("exp1_done"), sem("p1_done")
        s2_ready, max2_done, exp2_done, p2_done = sem("s2_ready"), sem("max2_done"), sem("exp2_done"), sem("p2_done")
        p1t_ready, p1t_done = sem("p1t_ready"), sem("p1t_done")
        p2t_ready, p2t_done, s2c_ready, s2c_done = sem("p2t_ready"), sem("p2t_done"), sem("s2c_ready"), sem("s2c_done")
        ct_ready, ct_done, st_ready, st_done = sem("ct_ready"), sem("ct_done"), sem("st_ready"), sem("st_done")
        mix_ready, eg_done, s2_done, x_done = sem("mix_ready"), sem("exp_gate_done"), sem("s2_done"), sem("x_done")
        block = ctx.enter_context(nc.Block())
        scale = float(D) ** -0.5

        @block.sync
        def _(sp):
            sp.dma_start(W[:], k.ins["w_a2"]).then_inc(loaded, 16)
            sp.dma_start(WG[:], k.ins["wg_a2"]).then_inc(loaded, 16)
            sp.dma_start(bt[:], k.ins["bt_a2"]).then_inc(loaded, 16)
            sp.dma_start(br[:], k.ins["br_a2"].unsqueeze(0)).then_inc(loaded, 16)
            sp.wait_ge(loaded, 64)

        @block.gpsimd
        def _(pool):
            for i, w in enumerate((QC, KCH, VC)):
                pool.wait_ge(whi, i + 1)
                nc.gpsimd.tensor_tensor(Wl[:, i], W[:, w], Wh[:, i].bitcast(F32), ALU.subtract).then_inc(wl_done, 1)

        @block.scalar
        def _(act):
            act.wait_ge(loaded, 64)
            for i, w in enumerate((QC, KCH, VC)):
                nc.scalar.activation(Wh[:, i], W[:, w], ACT.Copy).then_inc(whi, 1)
            act.wait_ge(ctx_ready, 1)
            for c in range(KC):
                nc.scalar.activation(ksT[:, c], ps[:, 2, c * 256:(c + 1) * 256], ACT.Identity,
                                     bias=bt[:, 1, c:c + 1]).then_inc(ctx_done, 1)
                nc.scalar.activation(qsT[:, c], ps[:, 3, c * 256:(c + 1) * 256], ACT.Identity,
                                     bias=bt[:, 2, c:c + 1]).then_inc(ctx_done, 1)
            for b in range(B):
                norm.act_evacuate(act, b, 0)
                act.wait_ge(q_ready, b + 1)
                for c in range(KC):
                    nc.scalar.activation(qT[:, c], ps[:, c, :], ACT.Identity, bias=bt[:, 0, c:c + 1]).then_inc(q_done, 1)
                act.wait_ge(k_ready, b + 1)
                for c in range(KC):
                    nc.scalar.activation(kcT[:, c], ps[:, c, :], ACT.Identity, bias=bt[:, 3, c:c + 1]).then_inc(k_done, 1)
                act.wait_ge(sub_done, b + 1)
                nc.scalar.activation(e1[:], e1[:], ACT.Exp, scale=scale).then_inc(exp1_done, 1)
                act.wait_ge(v_ready, b + 1)
                nc.scalar.activation(vc[:], ps[:, 2:4, :].rearrange("p a (t d) -> p (a t) d", t=2),
                                     ACT.Copy).then_inc(v_done, 1)
                act.wait_ge(max2_done, b + 1)
                nc.scalar.activation(e2[:], ps[0:SK, 5, :], ACT.Exp, scale=scale, bias=m2[:],
                                     accum_out=r2[:]).then_inc(exp2_done, 1)
                act.wait_ge(p1t_ready, b + 1)
                nc.scalar.activation(p1T[:], ps[0:SK, 4, :], ACT.Copy).then_inc(p1t_done, 1)
                act.wait_ge(p2t_ready, b + 1)
                nc.scalar.activation(p2T[:], ps[:, 5, 0:TB * SK].rearrange("p (t s) -> p t s", t=TB),
                                     ACT.Copy).then_inc(p2t_done, 1)
                act.wait_ge(ct_ready, b + 1)
                nc.scalar.activation(cT[:], ps[:, 2:4, :], ACT.Copy).then_inc(ct_done, 1)
                act.wait_ge(st_ready, b + 1)
                nc.scalar.activation(sT[:], ps[:, 2:4, :], ACT.Copy).then_inc(st_done, 1)
                for i in range(TB):
                    t = b * TB + i
                    act.wait_ge(mix_ready, t + 1)
                    if t >= 2:
                        act.wait_ge(x_done, t - 1)
                    nc.scalar.activation(g[:, t % 2], ps[:, 6, 0:D], ACT.Exp, scale=-1.0).then_inc(eg_done, 1)
                    nc.scalar.activation(s2[:, t % 2], ps[:, 7, D:2 * D], ACT.Copy).then_inc(s2_done, 1)

        @block.vector
        def _(dve):
            ch = Chain(dve, dstep)
            norm.dve_norm(dve, 0)
            for b in range(B):
                if b < B:
                    dve.wait_ge(vs_ready, b + 1)
                    nc.vector.tensor_copy(vs[:, b], ps[0:SK, 6 + b % 2, 0:D]).then_inc(vs_done, 1)
            norm.dve_low(dve, 0, 0)
            norm.dve_norm(dve, 1)
            for b in range(B):
                dve.wait_ge(s1_ready, b + 1)
                sc = ps[:, 4, 0:TB * SK].rearrange("p (t s) -> p t s", t=TB)
                ch.link(nc.vector.tensor_reduce(m1[:], sc, AX.X, ALU.max))
                nc.vector.tensor_tensor(e1[:], sc, m1[:].unsqueeze(2).to_broadcast([P, TB, SK]),
                                        ALU.subtract).then_inc(sub_done, 1)
                dve.wait_ge(s2_ready, b + 1)
                ch.link(nc.vector.tensor_reduce(m2[:], ps[0:SK, 5, :], AX.X, ALU.max))
                nc.vector.tensor_scalar(m2[:], m2[:], -scale, None, ALU.mult).then_inc(max2_done, 1)
                dve.wait_ge(exp1_done, b + 1)
                ch.link(nc.vector.tensor_reduce(r1[:], e1[:], AX.X, ALU.add))
                ch.link(nc.vector.reciprocal(r1[:], r1[:]))
                nc.vector.tensor_tensor(e1[:], e1[:], r1[:].unsqueeze(2).to_broadcast([P, TB, SK]),
                                        ALU.mult).then_inc(p1_done, 1)
                dve.wait_ge(exp2_done, b + 1)
                ch.link(nc.vector.reciprocal(r2[:], r2[:]))
                nc.vector.tensor_scalar(e2[:], e2[:], r2[:], None, ALU.mult).then_inc(p2_done, 1)
                dve.wait_ge(s2c_ready, b + 1)
                nc.vector.tensor_copy(s2c[:], ps[0:SK, 4, 0:D]).then_inc(s2c_done, 1)
                if b + 2 < B:
                    norm.dve_norm(dve, b + 2)
                for i in range(TB):
                    t = b * TB + i
                    dve.wait_ge(eg_done, t + 1)
                    gt, dt = g[:, t % 2], df[:, t % 2]
                    ch.link(nc.vector.tensor_scalar(gt, gt, 1.0, None, ALU.add))
                    ch.add(nc.vector.reciprocal(gt, gt))
                    dve.wait_ge(s2_done, t + 1)
                    ch.link(nc.vector.tensor_tensor(dt, ps[:, 7, 0:D], s2[:, t % 2], ALU.subtract))
                    ch.link(nc.vector.tensor_tensor(dt, dt, gt, ALU.mult))
                    ch.link(nc.vector.tensor_tensor(dt, dt, s2[:, t % 2], ALU.add))
                    nc.vector.scalar_tensor_tensor(k.X[:, t, :], dt, gate, k.X[:, t, :], ALU.mult,
                                                   ALU.add).then_inc(x_done, 1)
                if b + 1 < B:
                    norm.dve_low(dve, b + 1, 0)

        @block.tensor
        def _(pe):
            ones = k.cst[0:1, C_ONE:C_ONE + P]
            interp = k.cst[0:SK, C_INT:C_INT + S]
            pe.wait_ge(loaded, 64)
            for w, bank in ((KS, 2), (QS, 3)):
                for c in range(KC):
                    for j in range(KC):
                        last = nc.tensor.matmul(ps[:, bank, c * 256:(c + 1) * 256], W[:, w, j, c * P:(c + 1) * P],
                                                k.ctxT[:, j, :], start=(j == 0), stop=(j == KC - 1))
            last.then_inc(ctx_ready, 1)
            norm.pe_transpose(pe, 0, 0)
            for b in range(B):
                if b >= 2:
                    pe.wait_ge(vs_done, b - 1)
                for j in range(KC):
                    nc.tensor.matmul(ps[0:SK, 6 + b % 2, 0:D], k.ctxT[:, j, b * SK:(b + 1) * SK], W[:, VS, j],
                                     start=(j == 0), stop=False)
                nc.tensor.matmul(ps[0:SK, 6 + b % 2, 0:D], ones[:, 0:SK], br[:, 0:D], start=False,
                                 stop=True).then_inc(vs_ready, 1)

            def project(i, b):
                for c in range(KC):
                    for j in range(KC):
                        last = matmul3(nc, ps[:, c, :], Wh[:, i, j, c * P:(c + 1) * P], Wl[:, i, j, c * P:(c + 1) * P],
                                       norm.xh[:, b % 2, j], norm.xl[:, b % 2, j], j == 0, j == KC - 1)
                return last

            for b in range(B):
                ctx_cols = slice(b * SK, (b + 1) * SK)
                if b:
                    pe.wait_ge(k_done, KC * b)
                    norm.pe_transpose(pe, b, 0)
                pe.wait_ge(norm.xl_done, b + 1)
                if b == 0:
                    pe.wait_ge(wl_done, 3)
                    pe.wait_ge(ctx_done, 4)
                project(0, b).then_inc(q_ready, 1)
                if b:
                    pe.wait_ge(st_done, b)
                for t in range(TB):
                    out = ps[:, 2 + t // 2, (t % 2) * D:(t % 2 + 1) * D]
                    q = slice(t * P, (t + 1) * P)
                    for j in range(KC):
                        matmul3(nc, out, norm.xh[:, b % 2, j, q], norm.xl[:, b % 2, j, q], Wh[:, 2, j], Wl[:, 2, j],
                                j == 0, False)
                    last = nc.tensor.matmul(out, ones, br[:, D:2 * D], start=False, stop=True)
                last.then_inc(v_ready, 1)
                pe.wait_ge(q_done, KC * (b + 1))
                project(1, b).then_inc(k_ready, 1)
                if b:
                    pe.wait_ge(s2c_done, b)
                for t in range(TB):
                    for j in range(KC):
                        last = nc.tensor.matmul(ps[:, 4, t * SK:(t + 1) * SK], qT[:, j, t * P:(t + 1) * P],
                                                ksT[:, j, ctx_cols], start=(j == 0), stop=(j == KC - 1))
                last.then_inc(s1_ready, 1)
                pe.wait_ge(k_done, KC * (b + 1))
                if b:
                    pe.wait_ge(p2t_done, b)
                for j in range(KC):
                    last = nc.tensor.matmul(ps[0:SK, 5, :], qsT[:, j, ctx_cols], kcT[:, j], start=(j == 0),
                                            stop=(j == KC - 1))
                last.then_inc(s2_ready, 1)
                pe.wait_ge(p1_done, b + 1)
                for t in range(TB):
                    last = nc.tensor.transpose(ps[0:SK, 4, t * P:(t + 1) * P], e1[:, t, :], k.ident)
                last.then_inc(p1t_ready, 1)
                pe.wait_ge(p2_done, b + 1)
                for t in range(TB):
                    last = nc.tensor.transpose(ps[:, 5, t * SK:(t + 1) * SK], e2[:, t * P:(t + 1) * P],
                                               k.ident[0:SK, 0:SK])
                last.then_inc(p2t_ready, 1)
                pe.wait_ge(p1t_done, b + 1)
                pe.wait_ge(v_done, b + 1)
                for c in range(KC):
                    last = nc.tensor.matmul(ps[:, 2 + c, :], vs[:, b, c * P:(c + 1) * P], p1T[:], start=True, stop=True)
                last.then_inc(ct_ready, 1)
                pe.wait_ge(p2t_done, b + 1)
                for t in range(TB):
                    last = nc.tensor.matmul(ps[0:SK, 4, 0:D], p2T[:, t], vc[:, t], start=(t == 0), stop=(t == TB - 1))
                last.then_inc(s2c_ready, 1)
                pe.wait_ge(s2c_done, b + 1)
                pe.wait_ge(ct_done, b + 1)
                for c in range(KC):
                    last = nc.tensor.matmul(ps[:, 2 + c, :], s2c[:, c * P:(c + 1) * P], interp, start=True, stop=True)
                last.then_inc(st_ready, 1)
                pe.wait_ge(st_done, b + 1)
                for i in range(TB):
                    t = b * TB + i
                    q = slice(i * P, (i + 1) * P)
                    if t == 0:
                        pe.wait_ge(vs_done, B)
                    else:
                        pe.wait_ge(x_done, t)
                    for c in range(4):
                        src = cT if c < 2 else sT
                        nc.tensor.matmul(ps[:, 6, 0:D], src[:, c % 2, q], WG[:, c], start=(c == 0), stop=False)
                    nc.tensor.matmul(ps[:, 6, 0:D], ones, br[:, 2 * D:3 * D], start=False, stop=True)
                    nc.tensor.matmul(ps[:, 7, 0:D], p1T[:, q], vs[:, b], start=True, stop=True)
                    nc.tensor.matmul(ps[:, 7, D:2 * D], interp[:, q], s2c[:], start=True, stop=True).then_inc(mix_ready, 1)


STAGES = [
    lambda k: attention16(k, 0), lambda k: experts_ffn(k, 0), window_attention, lambda k: experts_ffn(k, 1),
    two_way_attention, lambda k: experts_ffn(k, 2), lambda k: attention16(k, 3), dense_ffn,
]


def build(nc, ins, out, stages=range(8)):
    with ExitStack() as ctx:
        k = Core(nc, ctx, ins, out)
        prologue(k)
        for s in stages:
            k.clear()
            STAGES[s](k)
        stored = k.sem("stored")
        block = ctx.enter_context(nc.Block())

        @block.sync
        def _(sp):
            sp.dma_start(out.rearrange("(t p) d -> p t d", p=P), k.X[:]).then_inc(stored, 16)
            sp.wait_ge(stored, 16)


def _window_counts():
    import numpy as np

    keys = list(range(11)) + [SK - 1]
    counts = np.zeros((S, 12), np.float32)
    for t in range(S):
        near = [i for i in range(-4, 4) if 0 <= t + i < S]
        while len(near) < 8:
            if t + len(near) < S:
                near.append(t + len(near))
            else:
                near.insert(0, t - (8 - len(near)))
        for p in near:
            counts[t, keys.index(min(p % S, SK - 1))] += 1
    return counts


def _constants():
    import numpy as np

    c = np.zeros((P, NC), np.float32)
    p = np.arange(P)
    c[:, C_ID:C_ID + P] = np.eye(P)
    c[:, C_TRI:C_TRI + P] = p[:, None] < p[None, :]
    c[:, C_ONE:C_ONE + P] = 1
    c[:, C_HB16:C_HB16 + 8] = p[:, None] // 16 == np.arange(8)
    c[:, C_HB32:C_HB32 + 4] = p[:, None] // 32 == np.arange(4)
    c[:, C_REV:C_REV + 9] = 16 - np.arange(9)
    c[:, C_J:C_J + 40] = np.arange(40)
    c[:, C_WB:C_WB + 8] = p[:, None] // 12 == np.arange(8)
    counts = _window_counts().reshape(TB, P, 12).transpose(1, 0, 2).reshape(P, TB * 12)
    c[:, C_CNT:C_CNT + 48] = counts
    c[:, C_WBIAS:C_WBIAS + 48] = np.where(counts > 0, 0, -1e30)
    pos = np.clip((np.arange(S) + 0.5) * (SK / S) - 0.5, 0, SK - 1)
    lo = np.floor(pos).astype(int)
    hi = np.minimum(lo + 1, SK - 1)
    m = np.zeros((SK, S), np.float32)
    m[lo, np.arange(S)] += 1 - (pos - lo)
    m[hi, np.arange(S)] += pos - lo
    c[:SK, C_INT:C_INT + S] = m
    return c


def _arrays(i):
    import numpy as np

    a = lambda n: np.asarray(i[n])
    kmaj = lambda w: w.T.reshape(-1, P, w.shape[0]).transpose(1, 0, 2)
    feat = lambda v: v.reshape(KC, P).T
    out = {
        "x": a("x").reshape(B * S, D), "cst": _constants(), "g_xattn": a("g_xattn"), "g_ffn": a("g_ffn"),
        "ctxT": a("ctx_1024").reshape(B * SK, D).T.reshape(KC, P, B * SK).transpose(1, 0, 2),
        "mask_q": a("mask_Bx1xSxS2_if1").reshape(B * S, SK), "mask_k": a("mask_Bx1xS2_if1").reshape(B, SK),
        "w_a0": np.stack([kmaj(a(f"L0_xattn_W{c}")) for c in "qkvo"], 1), "bo_a0": a("L0_xattn_bo"),
        "w_a3": np.stack([kmaj(a(f"L3_xattn_W{c}")) for c in "qkvo"], 1), "bo_a3": a("L3_xattn_bo"),
        "bqk_a3": np.stack([feat(a("L3_xattn_bq")), feat(a("L3_xattn_bk"))], 1), "bv_a3": a("L3_xattn_bv"),
        "w_a1": np.stack([kmaj(w) for w in (*a("L1_xattn_in_proj_w").reshape(3, D, D), a("L1_xattn_out_w"))], 1),
        "bqk_a1": np.stack([feat(a("L1_xattn_in_proj_b")[:D]), feat(a("L1_xattn_in_proj_b")[D:2 * D])], 1),
        "bv_a1": a("L1_xattn_in_proj_b")[2 * D:], "bo_a1": a("L1_xattn_out_b"),
        "w_a2": np.stack([kmaj(a(f"L2_xattn_W{n}")) for n in ("q_c", "k_s", "v_s", "q_s", "k_c", "v_c")], 1),
        "wg_a2": kmaj(a("L2_xattn_Wg")),
        "bt_a2": np.stack([feat(a(f"L2_xattn_b{n}")) for n in ("q_c", "k_s", "q_s", "k_c")], 1),
        "br_a2": np.concatenate([a("L2_xattn_bv_s"), a("L2_xattn_bv_c"), a("L2_xattn_bg")]),
    }

    def experts(gate, up, down):
        n, hid, _ = gate.shape
        gu = np.concatenate([gate, up], 1).transpose(0, 2, 1).reshape(n, KC, P, 2 * hid).transpose(0, 2, 1, 3)
        chunks = -(-hid // P)
        dn = np.zeros((n, chunks * P, D), np.float32)
        dn[:, :hid] = down.transpose(0, 2, 1)
        dn = dn.reshape(n, chunks, P, D).transpose(0, 2, 1, 3)
        return np.concatenate([gu.reshape(n, P, -1), dn.reshape(n, P, -1)], 2)

    cat = lambda n, m: np.concatenate([a(n), a(m)], 0)
    guw = a("L2_ffn_gate_up_weight")
    out |= {
        "we_f0": experts(a("L0_ffn_we_gate"), a("L0_ffn_we_up"), a("L0_ffn_we_down")),
        "we_f1": experts(cat("L1_ffn_w1", "L1_ffn_new_w1"), cat("L1_ffn_w3", "L1_ffn_new_w3"),
                         cat("L1_ffn_w2", "L1_ffn_new_w2")),
        "we_f2": experts(guw[:, :704], guw[:, 704:], a("L2_ffn_down_weight")),
        "gate_f0": kmaj(a("L0_ffn_gate_w")), "gate_f2": kmaj(a("L2_ffn_router_weight")),
        "gate_f1": kmaj(cat("L1_ffn_gate_weight", "L1_ffn_new_gate_weight")),
        "gbias_f1": np.concatenate([np.zeros(8, np.float32), a("L1_ffn_gate_bias")]),
        "nw_f2": a("L2_ffn_norm_weight"), "alpha_f2": a("L2_ffn_residual_alpha").reshape(1),
        "wd_f0": np.concatenate([kmaj(a("L0_ffn_ws_gate")), kmaj(a("L0_ffn_ws_up"))], 2),
        "wo_f0": kmaj(a("L0_ffn_ws_down")),
        "wd_f3": np.concatenate([kmaj(a("L3_ffn_w_gate")), kmaj(a("L3_ffn_w_up"))], 2),
        "wo_f3": kmaj(a("L3_ffn_w_down")),
    }
    return {n: np.ascontiguousarray(v) for n, v in out.items()}


def kernel(**inputs):
    import concourse.bacc as bacc
    from concourse.bass_utils import run_bass_kernel_spmd

    nc = bacc.Bacc("TRN2", target_bir_lowering=False, num_devices=1)
    arrays = _arrays(inputs)
    aps = {n: nc.dram_tensor(f"in_{n}", v.shape, mybir.dt.from_np(v.dtype), kind="ExternalInput").ap()
           for n, v in arrays.items()}
    out = nc.dram_tensor("out_x", (B * S, D), F32, kind="ExternalOutput").ap()
    build(nc, aps, out)
    r = run_bass_kernel_spmd(nc, [{f"in_{n}": v for n, v in arrays.items()}], core_ids=[0])
    return r.results[0]["out_x"].reshape(B, S, D)
```
